# Optimizing a Trainium2 kernel written in Bass

```python
import numpy as np
import jax
import jax.numpy as jnp

def _softmax(x, axis=-1):
    return jax.nn.softmax(x, axis=axis)

def _gelu(x):
    return jax.nn.gelu(x, approximate=True)

def _silu(x):
    return jax.nn.silu(x)

def _sigmoid(x):
    return jax.nn.sigmoid(x)

def _layernorm(x, axis=-1, eps=1e-05):
    m = jnp.mean(x, axis=axis, keepdims=True)
    v = jnp.var(x, axis=axis, keepdims=True)
    return (x - m) / jnp.sqrt(v + eps)

def _scatter_add(tgt, idx, src, axis=0):
    return tgt.at[idx].add(src)

def _segment_sum(src, seg, n):
    return jax.ops.segment_sum(src, seg, n)
kernel_name = 'mk_macaron_d1_jaxref_r4_1d248c'

def setup_inputs(seed: int=0):
    np.random.seed(seed)
    _w = jnp.asarray

    def _L0_attn_setup():
        import jax, jax.numpy as jnp
        import numpy as np
        import math
        B, S, D = (4, 512, 256)
        H = 16
        HD = D // H
        DL = 64
        LAMBDA_DECAY = 0.01
        key = jax.random.key(seed)
        ks = jax.random.split(key, 8)
        sc = lambda fan_in: 1.0 / math.sqrt(fan_in)
        return {'x': jax.random.normal(ks[0], (B, S, D), dtype=jnp.float32), 'W_q': jax.random.normal(ks[1], (D, D), dtype=jnp.float32) * sc(D), 'W_k': jax.random.normal(ks[2], (D, D), dtype=jnp.float32) * sc(D), 'W_v': jax.random.normal(ks[3], (D, D), dtype=jnp.float32) * sc(D), 'W_o': jax.random.normal(ks[4], (D, D), dtype=jnp.float32) * sc(D), 'W_down_kv': jax.random.normal(ks[5], (D, DL), dtype=jnp.float32) * sc(D), 'W_up_k': jax.random.normal(ks[6], (DL, D), dtype=jnp.float32) * sc(DL), 'W_up_v': jax.random.normal(ks[7], (DL, D), dtype=jnp.float32) * sc(DL)}
    _L0_attn_in = _L0_attn_setup()

    def _L0_ffn_setup():
        import jax, jax.numpy as jnp
        import numpy as np
        EMBED = 256
        NUM_EXPERTS = 8
        TOP_K = 2
        key = jax.random.key(seed)
        ks = jax.random.split(key, 6)
        scale = EMBED ** (-0.5)
        return {'x': jax.random.normal(ks[0], (4, 1024, EMBED), jnp.float32), 'router_w': jax.random.normal(ks[1], (EMBED, NUM_EXPERTS), jnp.float32) * scale, 'router_b': jnp.zeros((NUM_EXPERTS,), jnp.float32), 'we_gate': jax.random.normal(ks[2], (NUM_EXPERTS, EMBED, EMBED), jnp.float32) * scale, 'we_up': jax.random.normal(ks[3], (NUM_EXPERTS, EMBED, EMBED), jnp.float32) * scale, 'we_down': jax.random.normal(ks[4], (NUM_EXPERTS, EMBED, EMBED), jnp.float32) * scale}
    _L0_ffn_in = _L0_ffn_setup()
    _d = {'L0_attn_x': _L0_attn_in['x'], 'L0_attn_W_q': _L0_attn_in['W_q'], 'L0_attn_W_k': _L0_attn_in['W_k'], 'L0_attn_W_v': _L0_attn_in['W_v'], 'L0_attn_W_o': _L0_attn_in['W_o'], 'L0_attn_W_down_kv': _L0_attn_in['W_down_kv'], 'L0_attn_W_up_k': _L0_attn_in['W_up_k'], 'L0_attn_W_up_v': _L0_attn_in['W_up_v'], 'L0_ffn_router_w': _L0_ffn_in['router_w'], 'L0_ffn_router_b': _L0_ffn_in['router_b'], 'L0_ffn_we_gate': _L0_ffn_in['we_gate'], 'L0_ffn_we_up': _L0_ffn_in['we_up'], 'L0_ffn_we_down': _L0_ffn_in['we_down']}
    _x0 = _d['L0_attn_x']
    _d['L0_attn_x'] = jax.random.normal(jax.random.fold_in(jax.random.key(seed), 1), (16, 1024, 256), dtype=_x0.dtype)
    del _x0
    return _d

def reference(L0_attn_x, L0_attn_W_q, L0_attn_W_k, L0_attn_W_v, L0_attn_W_o, L0_attn_W_down_kv, L0_attn_W_up_k, L0_attn_W_up_v, L0_ffn_router_w, L0_ffn_router_b, L0_ffn_we_gate, L0_ffn_we_up, L0_ffn_we_down):

    def _L0_attn_ref(x, W_q, W_k, W_v, W_o, W_down_kv, W_up_k, W_up_v):
        import jax, jax.numpy as jnp
        import numpy as np
        import math
        B, S, D = (4, 512, 256)
        H = 16
        HD = D // H
        DL = 64
        LAMBDA_DECAY = 0.01
        b, s, d = x.shape
        q = x @ W_q
        k = x @ W_k
        v = x @ W_v
        latent_kv = (k + v) @ W_down_kv
        k_rec = (latent_kv @ W_up_k).reshape(b, s, H, HD).transpose(0, 2, 1, 3)
        v_rec = (latent_kv @ W_up_v).reshape(b, s, H, HD).transpose(0, 2, 1, 3)
        qh = q.reshape(b, s, H, HD).transpose(0, 2, 1, 3)
        scores = jnp.einsum('bhqd,bhkd->bhqk', qh, k_rec) / math.sqrt(d)
        t = jnp.arange(s, dtype=jnp.float32)
        decay = jnp.exp(-LAMBDA_DECAY * jnp.abs(t[:, None] - t[None, :]))
        scores = scores * decay[None, None, :, :]
        attn = jax.nn.softmax(scores, axis=-1)
        out = jnp.einsum('bhqk,bhkd->bhqd', attn, v_rec)
        out = out.transpose(0, 2, 1, 3).reshape(b, s, d)
        return out @ W_o

    def _L0_ffn_ref(x, router_w, router_b, we_gate, we_up, we_down):
        import jax, jax.numpy as jnp
        import numpy as np
        EMBED = 256
        NUM_EXPERTS = 8
        TOP_K = 2
        x_shape = x.shape
        x_flat = x.reshape(-1, x_shape[-1])
        num_tokens = x_flat.shape[0]
        router_logits = x_flat @ router_w + router_b
        topk_weights, topk_indices = jax.lax.top_k(router_logits, k=TOP_K)
        topk_weights = jax.nn.softmax(topk_weights, axis=-1)
        token_idx_mesh = jnp.repeat(jnp.arange(num_tokens), TOP_K)
        expert_idx_mesh = topk_indices.reshape(-1)
        sort_permutation = jnp.argsort(expert_idx_mesh)
        sorted_expert_idx = expert_idx_mesh[sort_permutation]
        sorted_token_idx = token_idx_mesh[sort_permutation]
        group_sizes = jnp.bincount(sorted_expert_idx, length=NUM_EXPERTS)
        sorted_tokens = x_flat[sorted_token_idx]
        ff_gate = jax.lax.ragged_dot(sorted_tokens, we_gate, group_sizes)
        ff_up = jax.lax.ragged_dot(sorted_tokens, we_up, group_sizes)
        activated = jax.nn.silu(ff_gate) * ff_up
        ff_out = jax.lax.ragged_dot(activated, we_down, group_sizes)
        sorted_weights = topk_weights.reshape(-1)[sort_permutation]
        ff_out = ff_out * sorted_weights[:, None]
        output_flat = jnp.zeros_like(x_flat).at[sorted_token_idx].add(ff_out)
        return output_flat.reshape(x_shape)
    x = L0_attn_x
    x = x + 0.5 * _L0_ffn_ref(_layernorm(x, axis=-1), L0_ffn_router_w, L0_ffn_router_b, L0_ffn_we_gate, L0_ffn_we_up, L0_ffn_we_down)
    x = x + _L0_attn_ref(_layernorm(x, axis=-1), L0_attn_W_q, L0_attn_W_k, L0_attn_W_v, L0_attn_W_o, L0_attn_W_down_kv, L0_attn_W_up_k, L0_attn_W_up_v)
    x = x + 0.5 * _L0_ffn_ref(_layernorm(x, axis=-1), L0_ffn_router_w, L0_ffn_router_b, L0_ffn_we_gate, L0_ffn_we_up, L0_ffn_we_down)
    return x

_drawn_inputs = setup_inputs


def setup_inputs(seed=0):
    import zlib

    import numpy as np

    out = dict(_drawn_inputs(seed))
    spreads = {'L0_ffn_router_b': (0.0, 0.1)}
    factors = {}
    for name, (base, spread) in spreads.items():
        noise = np.random.default_rng([zlib.crc32(name.encode()), seed]).standard_normal(out[name].shape)
        drawn = base * np.exp(spread * noise) if base else spread * noise
        out[name] = jnp.asarray(drawn.astype(out[name].dtype))
    for name, factor in factors.items():
        out[name] = (out[name] * factor).astype(out[name].dtype)
    return out
```

```python
import concourse.bass as bass
from concourse import mybir
from contextlib import ExitStack
import numpy as np

F32 = mybir.dt.float32
BF16 = mybir.dt.bfloat16
I32 = mybir.dt.int32
U32 = mybir.dt.uint32
ACT = mybir.ActivationFunctionType
ALU = mybir.AluOpType
AX = mybir.AxisListType

D = 256
S = 1024
H = 16
HD = 16
DL = 64
E = 8
LAM = 0.01
EPS = 1e-5
NS = 9
NP = 6


class Queue:

    def __init__(self, sem):
        self.sem, self.n, self.items, self.seen, self.hold = sem, 0, [], {}, []

    def do(self, f, *after, mark=True):
        waits = []
        after, self.hold = [*self.hold, *after], []
        for tok in after:
            if tok is None:
                continue
            s, v, key = tok
            if self.seen.get(key, 0) < v:
                self.seen[key] = v
                waits.append((s, v))
        tok = None
        if mark:
            self.n += 1
            tok = (self.sem, self.n, id(self.sem))
        self.items.append((waits, f, (self.sem, 1) if mark else None))
        return tok

    def dma(self, stream, out, in_, *after):
        self.do(lambda e: e.dma_start(out, in_), *after, mark=False)
        waits, f, _ = self.items[-1]
        self.items[-1] = (waits, f, (stream.sem, 16))
        return stream.count()

    def last(self):
        return (self.sem, self.n, id(self.sem)) if self.n else None

    def run(self, eng):
        for waits, f, inc in self.items:
            for s, v in waits:
                eng.wait_ge(s, v)
            ins = f(eng)
            if inc:
                ins.then_inc(*inc)


class Stream:

    def __init__(self, sem):
        self.sem, self.n = sem, 0

    def count(self):
        self.n += 16
        return self.last()

    def last(self):
        return (self.sem, self.n, id(self.sem)) if self.n else None


class Core:

    def __init__(self, nc, ctx):
        self.nc, self.ctx, self.streams = nc, ctx, []
        self.pe, self.dve, self.act, self.pool, self.sp = (
            Queue(self.sem(n)) for n in ("s_pe", "s_dve", "s_act", "s_pool", "s_sp"))
        ps = ctx.enter_context(nc.psum_tensor("psum", [128, 4096], F32))
        self.bank = [ps[:, 512 * i:512 * i + 512] for i in range(8)]
        self.A = self.bank[0:2]
        self.T = [ps[:, 1024:2048], ps[:, 2048:3072]]
        self.V = ps[:, 3072:4096]
        self.a_n = 0
        self.a_free = [None, None]

    def sem(self, name):
        return self.ctx.enter_context(self.nc.semaphore(name))

    def stream(self, name):
        self.streams.append(Stream(self.sem(name)))
        return self.streams[-1]

    def unit(self, fill, use):
        i = self.a_n % 2
        self.a_n += 1
        tok = fill(self.A[i], self.a_free[i])
        self.a_free[i] = use(self.A[i], tok)

    def meet(self):
        at = [q.last() for q in (self.pe, self.dve, self.act, self.pool, self.sp)]
        at += [s.last() for s in self.streams]
        for q in (self.pe, self.dve, self.act, self.pool, self.sp):
            q.hold = at

    def mm(self, out, lhsT, rhs, *after, start=True, stop=True, mark=True):
        return self.pe.do(lambda e: e.matmul(out, lhsT, rhs, start=start, stop=stop), *after, mark=mark)

    def tr(self, out, in_, ident, *after, mark=True):
        return self.pe.do(lambda e: e.transpose(out, in_, ident), *after, mark=mark)


CAP = 16512
CB = CAP // 128
NBLK = 264


class Ring:

    def __init__(self, banks):
        self.banks, self.n, self.free = banks, 0, [None] * len(banks)

    def take(self):
        i = self.n % len(self.banks)
        self.n += 1
        return i, self.banks[i], self.free[i]


def moe(c, NT, xin, out, xs, ys, cst, w, begin, tag):
    nc, pe, dve, act, pool, sp = c.nc, c.pe, c.dve, c.act, c.pool, c.sp
    ctx = ExitStack()

    def sb(name, shape, dt=F32):
        return ctx.enter_context(nc.sbuf_tensor(tag + name, shape, dt))

    wgu = sb("wgu", [128, 2, E * 512])
    wdn = sb("wdn", [128, 2, E * D])
    rw = sb("rw", [128, 2, E])
    rb = sb("rb", [128, E])
    ident = sb("ident", [128, 128])
    tri = sb("tri", [128, 128], BF16)
    ones = sb("ones", [128, 128], BF16)
    trif = sb("trif", [128, 128])
    misc = sb("misc", [128, 8 + 8 + 1])
    iota8, ecap, iotap = misc[:, 0:8], misc[:, 8:16], misc[:, 16:17]
    jf = sb("jf", [1, NBLK])
    zero = sb("zero", [128, D])
    P = sb("P", [128, NT, 2])
    EX = sb("EX", [128, NT, 2])
    M = sb("M", [128, NT, 2])
    XB = 5
    X = sb("X", [128, XB, 4, D])
    xT = sb("xT", [128, 2, 2, 512])
    st = sb("st", [128, 2, 4, 6])
    mv = sb("mv", [128, 2, 4, 2])
    ve = sb("ve", [128, 2, 4])
    sq = sb("sq", [128, 2, 4])
    rs = sb("rs", [128, 2, 4])
    lg = sb("lg", [128, 2, 4, E])
    m8 = sb("m8", [128, 2, 4, 8])
    i8 = sb("i8", [128, 2, 4, 8], U32)
    OH = sb("OH", [128, 2, 4, 2, E])
    O = sb("O", [128, 2, 4, E], BF16)
    base = sb("base", [128, 2, E])
    rk = sb("rk", [128, 2, 4, E])
    pr = sb("pr", [128, 2, 4, 2, E])
    idx = sb("idx", [128, XB, 4, 2], U32)
    s_w, s_wb, s_pad = (c.stream(tag + n) for n in ("w", "wb", "pad"))
    s_ld = [c.stream(f"{tag}ld{i}") for i in range(XB)]
    s_sc = [c.stream(f"{tag}sc{i}") for i in range(XB)]

    def dv(f, *after):
        return dve.do(f, *after)

    ldc = None
    for dst, src in ((ident[:], cst["ident"]), (trif[:], cst["tri"]), (misc[:], cst["misc"]), (jf[:], cst["jf"]),
                     (rw[:], w["rw"].rearrange("(k p) n -> p k n", p=128)),
                     (rb[:], w["rb"].rearrange("(o n) -> o n", o=1).to_broadcast([128, E]))):
        ldc = sp.dma(s_w, dst, src, *begin)
    k1 = dv(lambda e: e.tensor_copy(tri[:], trif[:]), ldc)
    k2 = dv(lambda e: e.memset(ones[:], 1.0))
    k3 = dv(lambda e: e.memset(zero[:], 0.0))
    bt = dv(lambda e: e.tensor_copy(base[:, 0, :], ecap), ldc)
    setup = bt

    xv = xin.rearrange("(g t p) d -> g p t d", p=128, t=4)
    ov = out.rearrange("(g t p) d -> g p t d", p=128, t=4)
    NG = NT // 4
    ring = Ring(c.bank)
    okd = {}
    scat = {}
    loads = {}

    def load(g):
        loads[g] = sp.dma(s_ld[g % XB], X[:, g % XB], xv[g], scat.get(g - XB))
    for g in range(min(XB - 1, NG)):
        load(g)
    tb = {}
    for g in range(NG):
        z, xb = g % 2, g % XB
        pz = tb.get(g - 2)
        for t in range(4):
            a = dv(lambda e, t=t, z=z, xb=xb: e.bn_stats(st[:, z, t, :], X[:, xb, t, :]), loads[g], pz)
        for t in range(4):
            a2 = dv(lambda e, t=t, z=z: e.bn_aggr(mv[:, z, t, :], st[:, z, t, :]), a)
        a = dv(lambda e, z=z: e.tensor_scalar_add(ve[:, z, :], mv[:, z, :, 1], EPS), a2)
        q = act.do(lambda e, z=z: e.activation(sq[:, z, :], ve[:, z, :], ACT.Sqrt), a, pz)
        a = dv(lambda e, z=z: e.reciprocal(rs[:, z, :], sq[:, z, :]), q)
        a = dv(lambda e, z=z: e.tensor_tensor(sq[:, z, :], rs[:, z, :], rs[:, z, :], ALU.mult), a)
        a = dv(lambda e, z=z: e.tensor_tensor(sq[:, z, :], sq[:, z, :], ve[:, z, :], ALU.mult), a)
        a = dv(lambda e, z=z: e.tensor_scalar(sq[:, z, :], sq[:, z, :], -0.5, 1.5, ALU.mult, ALU.add), a)
        a = dv(lambda e, z=z: e.tensor_tensor(rs[:, z, :], rs[:, z, :], sq[:, z, :], ALU.mult), a)
        for t in range(4):
            xn = dv(lambda e, t=t, z=z, xb=xb: e.tensor_scalar(X[:, xb, t, :], X[:, xb, t, :], mv[:, z, t, 0:1],
                                                             rs[:, z, t:t + 1], ALU.subtract, ALU.mult), a)
        for k in range(2):
            i, bank, free = ring.take()
            for t in range(4):
                tok = c.tr(bank[:, 128 * t:128 * t + 128], X[:, xb, t, 128 * k:128 * k + 128], ident[:], xn, free, ldc)
            ring.free[i] = act.do(lambda e, k=k, z=z, bank=bank: e.activation(xT[:, z, k, :], bank, ACT.Copy),
                                  tok, okd.get(g - 2))
        xtd = ring.free[i]
        i, bank, free = ring.take()
        for t in range(4):
            for k in range(2):
                tok = c.mm(bank[:, E * t:E * t + E], xT[:, z, k, 128 * t:128 * t + 128], rw[:, k, :], xtd, free,
                           start=(k == 0), stop=(k == 1))
        okd[g] = tok
        a = ring.free[i] = dv(lambda e, z=z, bank=bank: e.tensor_tensor(
            lg[:, z], bank[:, 0:32].rearrange("p (t e) -> p t e", t=4),
            rb[:].rearrange("p (o e) -> p o e", o=1).to_broadcast([128, 4, E]), ALU.add), tok)
        for t in range(4):
            b1 = dv(lambda e, t=t, z=z: e.max(m8[:, z, t, :], lg[:, z, t, :]), a)
        for t in range(4):
            b2 = dv(lambda e, t=t, z=z: e.max_index(i8[:, z, t, :], m8[:, z, t, :], lg[:, z, t, :]), b1)
        dv(lambda e, z=z, g=g: e.tensor_copy(M[:, 4 * g:4 * g + 4, :], m8[:, z, :, 0:2]), b1)
        b3 = dv(lambda e, z=z, g=g: e.tensor_copy(EX[:, 4 * g:4 * g + 4, :], i8[:, z, :, 0:2]), b2)
        b4 = dv(lambda e, z=z, g=g: e.tensor_tensor(
            OH[:, z], EX[:, 4 * g:4 * g + 4, :].rearrange("p t (k o) -> p t k o", o=1).to_broadcast([128, 4, 2, E]),
            iota8.rearrange("p (a b e) -> p a b e", a=1, b=1).to_broadcast([128, 4, 2, E]), ALU.is_equal), b3)
        b5 = dv(lambda e, z=z: e.tensor_tensor(O[:, z], OH[:, z, :, 0, :], OH[:, z, :, 1, :], ALU.add), b4, tb.get(("pe", g - 2)))
        i, bank, free = ring.take()
        r4 = bank[:, 0:32].rearrange("p (t e) -> p t e", t=4)
        c.mm(r4, tri[:], O[:, z], b5, free, k1, k2, start=True, stop=False)
        for t in range(3):
            c.mm(r4[:, t + 1:4, :], ones[:], O[:, z, t:t + 1, :].to_broadcast([128, 3 - t, E]), start=False, stop=(t == 2))
        for t in range(4):
            tok = c.mm(bank[:, 32:40], ones[:], O[:, z, t, :], start=(t == 0), stop=(t == 3))
        tb[("pe", g)] = tok
        b6 = dv(lambda e, z=z, r4=r4: e.tensor_tensor(
            rk[:, z], r4, base[:, z].rearrange("p (o e) -> p o e", o=1).to_broadcast([128, 4, E]), ALU.add), tok, bt)
        bt = ring.free[i] = dv(lambda e, z=z, bank=bank: e.tensor_tensor(base[:, 1 - z], base[:, z], bank[:, 32:40], ALU.add),
                               b6)
        b7 = dv(lambda e, z=z: e.tensor_tensor(
            pr[:, z], OH[:, z], rk[:, z].rearrange("p t (o e) -> p t o e", o=1).to_broadcast([128, 4, 2, E]), ALU.mult), b6)
        b8 = dv(lambda e, z=z, g=g: e.tensor_reduce(P[:, 4 * g:4 * g + 4, :], pr[:, z], op=ALU.add, axis=AX.X), b7)
        b9 = dv(lambda e, g=g, xb=xb: e.tensor_copy(idx[:, xb], P[:, 4 * g:4 * g + 4, :]), b8, scat.get(g - XB))
        tb[g] = b9
        for t in range(4):
            for k in range(2):
                pool.do(lambda e, t=t, k=k, xb=xb: e.indirect_dma_start(
                    xs, bass.IndirectOffsetOnAxis(ap=idx[:, xb, t, k:k + 1], axis=0), X[:, xb, t, :], None),
                    b9, k3, *(begin if g == 0 else ()), mark=False)
                wts, f, _ = pool.items[-1]
                pool.items[-1] = (wts, f, (s_sc[xb].sem, 16))
                scat[g] = s_sc[xb].count()
        if g + XB - 1 < NG:
            load(g + XB - 1)
    wl = sp.dma(s_wb, wgu[:].rearrange("p k (e h n) -> p k e h n", e=E, h=2)[:, 0, :, 0, :],
                w["g"].rearrange("e (k p) n -> k p e n", p=128)[0])
    for k in range(2):
        if k:
            sp.dma(s_wb, wgu[:].rearrange("p k (e h n) -> p k e h n", e=E, h=2)[:, k, :, 0, :],
                   w["g"].rearrange("e (k p) n -> k p e n", p=128)[k])
        sp.dma(s_wb, wgu[:].rearrange("p k (e h n) -> p k e h n", e=E, h=2)[:, k, :, 1, :],
               w["u"].rearrange("e (k p) n -> k p e n", p=128)[k])
        wl = sp.dma(s_wb, wdn[:].rearrange("p k (e n) -> p k e n", e=E)[:, k],
                    w["d"].rearrange("e (k p) n -> k p e n", p=128)[k])

    zf = NG % 2
    cnt = sb("cnt", [128, E])
    nbi = sb("nbi", [128, E], I32)
    nb = sb("nb", [128, E])
    bend = sb("bend", [128, E])
    ysh = sb("ysh", [128, E])
    dl = sb("dl", [128, E])
    tot = sb("tot", [128, 1])
    padf = sb("padf", [128, E])
    padi = sb("padi", [128, E], U32)
    jt = sb("jt", [1, 4, NBLK])
    tabE = sb("tabE", [1, NBLK], I32)
    tabR = sb("tabR", [1, NBLK], I32)
    G = sb("G", [128, NT, 2])
    T1 = sb("T1", [128, NT, 2])
    yi = sb("yi", [128, NT, 2], U32)
    a = dv(lambda e: e.tensor_scalar(padf[:], base[:, zf], iotap, None, ALU.add), bt)
    padr = dv(lambda e: e.tensor_copy(padi[:], padf[:]), a)
    for x in range(E):
        pool.do(lambda e, x=x: e.indirect_dma_start(
            xs, bass.IndirectOffsetOnAxis(ap=padi[:, x:x + 1], axis=0), zero[:], None), padr, mark=False)
        wts, f, _ = pool.items[-1]
        pool.items[-1] = (wts, f, (s_pad.sem, 16))
        pads = s_pad.count()
    scattered = [s.last() for s in s_sc] + [pads]
    a = dv(lambda e: e.tensor_tensor(cnt[:], base[:, zf], ecap, ALU.subtract), bt)
    a = dv(lambda e: e.tensor_scalar_add(cnt[:], cnt[:], 127.0), a)
    a = dv(lambda e: e.tensor_copy(nbi[:], cnt[:]), a)
    a = dv(lambda e: e.tensor_single_scalar(nbi[:], nbi[:], 7, ALU.arith_shift_right), a)
    a = dv(lambda e: e.tensor_copy(nb[:], nbi[:]), a)
    a = dv(lambda e: e.tensor_copy(bend[:, 0:1], nb[:, 0:1]), a)
    for x in range(1, E):
        a = dv(lambda e, x=x: e.tensor_tensor(bend[:, x:x + 1], bend[:, x - 1:x], nb[:, x:x + 1], ALU.add), a)
    dv(lambda e: e.tensor_scalar_add(tot[:], bend[:, E - 1:E], -1.0), a)
    a = dv(lambda e: e.tensor_tensor(ysh[:], bend[:], nb[:], ALU.subtract), a)
    a = dv(lambda e: e.tensor_scalar_mul(ysh[:], ysh[:], 128.0), a)
    a = dv(lambda e: e.tensor_tensor(ysh[:], ysh[:], ecap, ALU.subtract), a)
    a = dv(lambda e: e.tensor_scalar(dl[:], nb[:], -1.0, float(CB), ALU.mult, ALU.add), a)
    a = dv(lambda e: e.tensor_scalar(jt[:, 0], jf[:], tot[0:1, :], None, ALU.min), a)
    dv(lambda e: e.tensor_copy(jt[:, 2], jt[:, 0]), a)
    a = dv(lambda e: e.memset(jt[:, 1], 0.0))
    for x in range(E - 1):
        a = dv(lambda e, x=x: e.tensor_scalar(jt[:, 3], jt[:, 0], bend[0:1, x:x + 1], None, ALU.is_ge), a)
        dv(lambda e: e.tensor_tensor(jt[:, 1], jt[:, 1], jt[:, 3], ALU.add), a)
        a = dv(lambda e, x=x: e.scalar_tensor_tensor(jt[:, 2], jt[:, 3], dl[0:1, x:x + 1], jt[:, 2], ALU.mult, ALU.add), a)
        a = dve.last()
    dv(lambda e: e.tensor_scalar_mul(jt[:, 3], jt[:, 2], 1.0), a)
    a = dve.last()
    dv(lambda e: e.tensor_copy(tabE[:], jt[:, 1]), a)
    tabs = dv(lambda e: e.tensor_copy(tabR[:], jt[:, 3]), a)
    for x in range(E):
        a = dv(lambda e, x=x: e.tensor_scalar(T1[:], EX[:], float(x), ysh[:, x:x + 1], ALU.is_equal, ALU.mult), a, dve.last())
        a = dv(lambda e: e.tensor_tensor(P[:], P[:], T1[:], ALU.add), a)
    rows = dv(lambda e: e.tensor_copy(yi[:], P[:]), a)
    a = dv(lambda e: e.tensor_tensor(G[:, :, 1], M[:, :, 1], M[:, :, 0], ALU.subtract), a)
    a = act.do(lambda e: e.activation(G[:, :, 1], G[:, :, 1], ACT.Exp), a)
    a = dv(lambda e: e.tensor_scalar(T1[:, :, 0], G[:, :, 1], 2.0, 2.0, ALU.mult, ALU.add), a, rows)
    a = dv(lambda e: e.reciprocal(G[:, :, 0], T1[:, :, 0]), a)
    gates = dv(lambda e: e.tensor_tensor(G[:, :, 1], G[:, :, 1], G[:, :, 0], ALU.mult), a)

    NX, NYB = 6, 4
    xb_ = X[:].rearrange("p a b d -> p (a b) d")
    xg, yb, sg, hb = xb_[:, 0:NX], xb_[:, NX:NX + NYB], xb_[:, 10:12], xb_[:, 12:14]
    xgT = sb("xgT", [128, 2, 256])
    hT = sb("hT", [128, 2, 256])
    s_xg = [c.stream(f"{tag}xg{i}") for i in range(NX)]
    s_yo = [c.stream(f"{tag}yo{i}") for i in range(NYB)]
    bk = c.bank
    tx = Ring([bk[0], bk[1]])
    gu = Ring([bk[2], bk[3]])
    th = Ring([bk[4], bk[5]])
    yk = Ring([bk[6], bk[7]])
    rE, rR = {}, {}
    n_tr = {}
    xl, xtd, gud, htd, hd, trh = {}, {}, {}, {}, {}, {}
    dwn = {}
    ydone = {}
    pe_regs = {}
    quiet = [dve.last(), act.last(), pe.last(), *scattered]

    def xload(j):
        def f(e):
            r = e.value_load(tabR[0:1, j:j + 1], min_val=0, max_val=8 * CB - 1)
            return e.dma_start(xg[:, j % NX], xs[bass.ds(r * 128, 128), :])
        sp.do(f, tabs, *quiet, n_tr.get(j - NX), mark=False)
        wts, f, _ = sp.items[-1]
        sp.items[-1] = (wts, f, (s_xg[j % NX].sem, 16))
        xl[j] = s_xg[j % NX].count()

    def trx(j):
        i, bank, free = tx.take()
        for k in range(2):
            tok = c.tr(bank[:, 128 * k:128 * k + 128], xg[:, j % NX, 128 * k:128 * k + 128], ident[:], xl[j], free, *quiet)
        n_tr[j] = tok
        tx.free[i] = xtd[j] = act.do(lambda e: e.activation(xgT[:, j % 2], bank[:, 0:256], ACT.Copy), tok, gud.get(j - 2))

    def gate_up(j):
        def f(e):
            r = e.value_load(tabE[0:1, j:j + 1], min_val=0, max_val=E - 1)
            rE[j] = r
            return None
        pe.do(f, tabs, mark=False)
        i, bank, free = gu.take()
        for k in range(2):
            tok = pe.do(lambda e, k=k, bank=bank: e.matmul(
                bank, xgT[:, j % 2, 128 * k:128 * k + 128], wgu[:, k, bass.ds(rE[j] * 512, 512)],
                start=(k == 0), stop=(k == 1)), xtd[j], free, wl)
        gud[j] = tok
        a = act.do(lambda e: e.activation(sg[:, j % 2], bank[:, 0:256], ACT.Silu), tok, hd.get(j - 2), quiet[2])
        hd[j] = gu.free[i] = dv(lambda e: e.tensor_tensor(hb[:, j % 2], sg[:, j % 2], bank[:, 256:512], ALU.mult), a,
                                trh.get(j - 2))

    def trh_(j):
        i, bank, free = th.take()
        for k in range(2):
            tok = c.tr(bank[:, 128 * k:128 * k + 128], hb[:, j % 2, 128 * k:128 * k + 128], ident[:], hd[j], free)
        trh[j] = tok
        th.free[i] = htd[j] = dv(lambda e: e.tensor_copy(hT[:, j % 2], bank[:, 0:256]), tok, dwn.get(j - 2))

    def down(j):
        i, bank, free = yk.take()
        for k in range(2):
            tok = pe.do(lambda e, k=k, bank=bank: e.matmul(
                bank[:, 0:D], hT[:, j % 2, 128 * k:128 * k + 128], wdn[:, k, bass.ds(rE[j] * D, D)],
                start=(k == 0), stop=(k == 1)), htd[j], free)
        dwn[j] = tok
        eng = act if j % 2 else dve
        cp = (lambda e: e.activation(yb[:, j % NYB], bank[:, 0:D], ACT.Copy)) if j % 2 else (
            lambda e: e.tensor_copy(yb[:, j % NYB], bank[:, 0:D]))
        a = yk.free[i] = eng.do(cp, tok, s_yo[j % NYB].last())
        ydone[j] = sp.dma(s_yo[j % NYB], ys[128 * j:128 * j + 128, :], yb[:, j % NYB], a)

    NB = min(NBLK, 2 * NT + 8)
    for j in range(min(NX, NB)):
        xload(j)
    trx(0)
    for j in range(NB + 2):
        if j < NB:
            gate_up(j)
        if 1 <= j < NB + 1:
            trh_(j - 1)
        if j + 1 < NB:
            trx(j + 1)
        if j >= 2:
            down(j - 2)
        if j + NX < NB:
            xload(j + NX)

    yall = [s.last() for s in s_yo]
    quiet = [dve.last(), act.last(), pe.last()]
    CBF = 3
    Xc = X[:, 0:CBF]
    Yg = sb("Yg", [128, CBF, 4, 2, D]) if False else None
    Y = sb("Y", [128, CBF, 8, D])
    s_cl = [c.stream(f"{tag}cl{i}") for i in range(CBF)]
    s_cg = [c.stream(f"{tag}cg{i}") for i in range(CBF)]
    s_co = [c.stream(f"{tag}co{i}") for i in range(CBF)]
    last = {}
    for g in range(NG):
        z = g % CBF
        ld = sp.dma(s_cl[z], Xc[:, z], xv[g], *quiet, *yall, s_co[z].last())
        for t in range(4):
            for k in range(2):
                pool.do(lambda e, t=t, k=k, g=g, z=z: e.indirect_dma_start(
                    Y[:, z, 2 * t + k, :], None, ys[0:128 * NB, :],
                    bass.IndirectOffsetOnAxis(ap=yi[:, 4 * g + t, k:k + 1], axis=0)), *yall, rows, last.get(g - CBF), mark=False)
                wts, f, _ = pool.items[-1]
                pool.items[-1] = (wts, f, (s_cg[z].sem, 16))
                got = s_cg[z].count()
        for t in range(4):
            a = dv(lambda e, t=t, z=z, g=g: e.scalar_tensor_tensor(
                Xc[:, z, t], Y[:, z, 2 * t], G[:, 4 * g + t, 0:1], Xc[:, z, t], ALU.mult, ALU.add), ld, got, gates)
        for t in range(4):
            a2 = dv(lambda e, t=t, z=z, g=g: e.scalar_tensor_tensor(
                Xc[:, z, t], Y[:, z, 2 * t + 1], G[:, 4 * g + t, 1:2], Xc[:, z, t], ALU.mult, ALU.add), a)
        last[g] = a2
        sp.dma(s_co[z], ov[g], Xc[:, z], a2)
    ctx.close()
    return [s.last() for s in s_co]


def attention(c, B, x1, x2, parts, mdram, cst, w):
    nc, pe, dve, act, pool, sp = c.nc, c.pe, c.dve, c.act, c.pool, c.sp
    ctx = ExitStack()

    def sb(name, shape, dt=F32):
        return ctx.enter_context(nc.sbuf_tensor("at_" + name, shape, dt))

    qst = sb("qst", [99, NS, 2, S], BF16)
    kst = sb("kst", [99, NS, 2, S], BF16)
    P = sb("P", [128, NP, S])
    NSD = 40
    Sd = sb("Sd", [128, NSD, 128])
    V = sb("V", [128, 2, 8, H, 17])
    XR = sb("XR", [128, 8, D])
    xT = sb("xT", [128, 2, S])
    lat = sb("lat", [DL, S])
    pt = sb("pt", [128, 2, 3, 512], BF16)
    qf = sb("qf", [128, 512])
    qv = sb("qv", [128, 2, 512])
    OT = sb("OT", [128, 8, D])
    OF = sb("OF", [128, 2, 512])
    Ou = sb("Ou", [128, S])
    res = sb("res", [128, 2, D])
    ident = sb("ident", [128, 128])
    decn = sb("decn", [128, S])
    decp = sb("decp", [128, S])
    Dm = sb("Dm", [128, 128])
    wq = sb("wq", [128, 2, D])
    wk = sb("wk", [128, 2, D])
    wo = sb("wo", [128, 2, D])
    wd = sb("wd", [128, 2, DL])
    wuk = sb("wuk", [DL, D])
    wuv = sb("wuv", [DL, D])
    wkT = Ou[:, 0:512].rearrange("p (k d) -> p k d", k=2)
    wkv = sb("wkv", [128, 2, DL])
    st = sb("st", [128, 6])
    mv = sb("mv", [128, 8, 2])
    ve = sb("ve", [128, 8])
    sq = sb("sq", [128, 8])
    rs = sb("rs", [128, 8])
    mx = sb("mx", [128, 2, 4, 8, 3])
    m = sb("m", [128, 2, 32])
    mT = sb("mT", [32, 128])
    mTr = sb("mTr", [32, 128])
    mp = sb("mp", [32, 3, 128], BF16)
    rc = sb("rc", [128, 4, 4])

    s_w, s_x, s_m, s_y = (c.stream("at_" + n) for n in ("w", "x", "m", "y"))
    s_pt = [c.stream(f"at_pt{i}") for i in range(2)]
    s_st = [c.stream(f"at_st{i}") for i in range(NS)]
    s_mr = [c.stream(f"at_mr{i}") for i in range(NS)]
    s_res = [c.stream(f"at_res{i}") for i in range(2)]
    s_yr = [c.stream(f"at_yr{i}") for i in range(2)]

    def fold(a):
        return a.rearrange("(k p) n -> p k n", p=128)

    for dst, src in ((ident[:], cst["ident"]), (decn[:], cst["decn"]), (decp[:], cst["decp"]),
                     (Dm[:], cst["dm"]), (wq[:], fold(w["q"])), (wk[:], fold(w["k"])),
                     (wkT, fold(w["v"])), (wd[:], fold(w["down"])), (wuk[:], w["upk"]),
                     (wuv[:], w["upv"]), (wo[:], fold(w["o"]))):
        loaded = sp.dma(s_w, dst, src)
    ones_k = dve.do(lambda e: e.memset(kst[96:99, :, :, :], 1.0))
    ones_v = dve.do(lambda e: e.memset(V[:, :, :, :, 16:17], 1.0))
    v0 = dve.do(lambda e: e.memset(c.V, 0.0))
    wsum = dve.do(lambda e: e.tensor_tensor(wk[:], wk[:], wkT, ALU.add), loaded)
    wqs = dve.do(lambda e: e.tensor_scalar_mul(wq[:], wq[:], 1.0 / 16.0), loaded)
    fT = {}
    for i in range(2):
        def fill(bank, free, i=i):
            for j in range(2):
                t = c.tr(bank[:, 128 * j:128 * j + 128], wk[:, i, 128 * j:128 * j + 128], ident[:],
                         wsum, loaded, free)
            return t

        def use(bank, tok, i=i):
            fT[i] = dve.do(lambda e: e.tensor_copy(
                Ou[:, 0:512].rearrange("p (j i q) -> p j i q", j=2, i=2)[:, :, i, :],
                bank[:, 0:256].rearrange("p (j q) -> p j q", j=2)), tok, wsum)
            return fT[i]
        c.unit(fill, use)

    def fill_wkv(bank, free):
        for i in range(2):
            for j in range(2):
                t = c.mm(bank[:, i * DL:(i + 1) * DL], Ou[:, 256 * j + 128 * i:256 * j + 128 * i + 128],
                         wd[:, j, :], fT[0], fT[1], free, start=(j == 0), stop=(j == 1))
        return t

    def use_wkv(bank, tok):
        return dve.do(lambda e: e.tensor_copy(wkv[:], bank[:, 0:128].rearrange("p (k n) -> p k n", k=2)), tok)
    c.unit(fill_wkv, use_wkv)
    setup = dve.last()

    xdone = {}
    vdone = {}
    pdone = {}
    vread = {}

    def prep(b):
        ld = sp.dma(s_x, XR[:], x1[b].rearrange("(t p) d -> p t d", p=128), pe.last() if b else None)
        for t in range(8):
            s1 = dve.do(lambda e, t=t: e.bn_stats(st[:], XR[:, t, :]), ld, dve.last())
            ag = dve.do(lambda e, t=t: e.bn_aggr(mv[:, t, :], st[:]), s1)
            if t % 3 == 2:
                yield
        a = dve.do(lambda e: e.tensor_scalar_add(ve[:], mv[:, :, 1], EPS), ag)
        a2 = act.do(lambda e: e.activation(sq[:], ve[:], ACT.Sqrt), a)
        a3 = dve.do(lambda e: e.reciprocal(rs[:], sq[:]), a2)
        n1 = dve.do(lambda e: e.tensor_tensor(sq[:], rs[:], rs[:], ALU.mult), a3)
        n2 = dve.do(lambda e: e.tensor_tensor(sq[:], sq[:], ve[:], ALU.mult), n1)
        n3 = dve.do(lambda e: e.tensor_scalar(sq[:], sq[:], -0.5, 1.5, ALU.mult, ALU.add), n2)
        n4 = dve.do(lambda e: e.tensor_tensor(rs[:], rs[:], sq[:], ALU.mult), n3)
        for t in range(8):
            xn = dve.do(lambda e, t=t: e.tensor_scalar(XR[:, t, :], XR[:, t, :], mv[:, t, 0:1], rs[:, t:t + 1],
                                                       ALU.subtract, ALU.mult), n4, ag)
            if t % 4 == 3:
                yield
        xTd = {}
        for ch in range(2):
            for k in range(2):
                def fill(bank, free, ch=ch, k=k):
                    for t in range(4):
                        tok = c.tr(bank[:, 128 * t:128 * t + 128], XR[:, 4 * ch + t, 128 * k:128 * k + 128],
                                   ident[:], xn, free)
                    return tok

                def use(bank, tok, ch=ch, k=k):
                    xTd[ch] = act.do(lambda e: e.activation(xT[:, k, 512 * ch:512 * ch + 512], bank[:], ACT.Copy),
                                     tok, prepd.get(b - 1))
                    return xTd[ch]
                c.unit(fill, use)
                yield
        latd = {}
        for ch in range(2):
            def fill(bank, free, ch=ch):
                for k in range(2):
                    tok = c.mm(bank[0:DL, :], wkv[:, k, :], xT[:, k, 512 * ch:512 * ch + 512], xTd[ch], setup, free,
                               start=(k == 0), stop=(k == 1))
                return tok

            def use(bank, tok, ch=ch):
                latd[ch] = act.do(lambda e: e.activation(lat[:, 512 * ch:512 * ch + 512], bank[0:DL, :], ACT.Copy), tok)
                return latd[ch]
            c.unit(fill, use)
            yield
        for kind in range(2):
            for hf in range(2):
                for ch in range(2):
                    def fill(bank, free):
                        sl = slice(512 * ch, 512 * ch + 512)
                        if kind == 0:
                            for k in range(2):
                                tok = c.mm(bank[:], wq[:, k, 128 * hf:128 * hf + 128], xT[:, k, sl], xTd[ch], wqs, free,
                                           start=(k == 0), stop=(k == 1))
                        else:
                            tok = c.mm(bank[:], wuk[:, 128 * hf:128 * hf + 128], lat[:, sl], latd[ch], free)
                        return tok

                    def use(bank, tok):
                        prev = st_pool.get("q")
                        st_pool["f"] = act.do(lambda e: e.activation(qf[:], bank[:], ACT.Copy), tok, prev)
                        return st_pool["f"]
                    c.unit(fill, use)
                    yield
                    for v in range(2):
                        dec = (decn, decp)[v]
                        z = v
                        dd = st_pool.get(("d", z))
                        a = pool.do(lambda e, v=v, dec=dec, ch=ch: e.tensor_tensor(
                            qv[:, v, :], qf[:], dec[:, 512 * ch:512 * ch + 512], ALU.mult), st_pool["f"], dve.last(), loaded,
                            st_pool.get(("c", z)))
                        a1 = dve.do(lambda e, v=v, z=z: e.tensor_copy(pt[:, z, 0, :], qv[:, v, :]), a, dd)
                        yield
                        a2 = pool.do(lambda e, v=v, z=z: e.tensor_tensor(qv[:, v, :], qv[:, v, :], pt[:, z, 0, :], ALU.subtract),
                                     a1)
                        a3 = dve.do(lambda e, v=v, z=z: e.tensor_copy(pt[:, z, 1, :], qv[:, v, :]), a2)
                        yield
                        a4 = pool.do(lambda e, v=v, z=z: e.tensor_tensor(pt[:, z, 2, :], qv[:, v, :], pt[:, z, 1, :],
                                                                       ALU.subtract), a3)
                        st_pool[("c", z)] = a4
                        st_pool["q"] = a4
                        for p in range(3):
                            dst = parts[b % 2, kind, 8 * hf:8 * hf + 8, p, :, v, 512 * ch:512 * ch + 512]
                            st_pool[("d", z)] = sp.dma(s_pt[z], dst, pt[:, z, p, :], a4, stfree.get(b - 2))
                        yield
        pdone[b] = [s_pt[0].last(), s_pt[1].last()]
        for t2 in range(4):
            def fill(bank, free):
                for j in range(2):
                    t = 2 * t2 + j
                    tok = c.mm(bank[:, 256 * j:256 * j + 256], lat[:, 128 * t:128 * t + 128], wuv[:], latd[t // 4], free)
                return tok

            def use(bank, tok):
                vdone[b] = act.do(lambda e, t2=t2, b=b: e.activation(
                    V[:, b % 2, 2 * t2:2 * t2 + 2, :, 0:16],
                    bank[:].rearrange("p (t h d) -> p t h d", t=2, h=H), ACT.Copy), tok, vread.get(b - 2))
                return vdone[b]
            c.unit(fill, use)
            yield
        prepd[b] = pe.last()

    prepd = {}
    st_pool = {}
    stfree = {}
    filled = {}
    qpat = ((0, 48), (48, 80), (80, 96))
    NH = B * H

    def fill_stack(n):
        b, h = divmod(n, H)
        s = n % NS
        free = tdone.get((n - NS) // 4) if n >= NS else None
        more = [*pdone[b], free]
        src = parts[b % 2]
        qd = qst[:, s, :, :]
        kd = kst[:, s, :, :]
        for p, (r0, r1) in enumerate(((0, 3), (3, 5), (5, 6))):
            for r in range(r0, r1):
                sp.dma(s_st[s], qd[16 * r:16 * r + 16], src[0, h, p], *more)
        sp.dma(s_st[s], kd[0:48], src[1, h].rearrange("p d v t -> (p d) v t"), *more)
        sp.dma(s_st[s], kd[48:80], src[1, h, 0:2].rearrange("p d v t -> (p d) v t"), *more)
        filled[n] = sp.dma(s_st[s], kd[80:96], src[1, h, 0], *more)
        if h == H - 1:
            stfree[b] = filled[n]

    tdone = {}
    sdfree = [None] * NSD
    sdlist = list(range(NSD))
    sdslot = {}
    sdtok = {}
    mrow = {}
    mdone = {}

    def pieces(t, c0, c1, diag_last):
        out = []
        if diag_last:
            left = [(0, 0, 128 * t, 0), (128 * t, 128 * t + 128, 896 - 128 * t, 1), (896, 128 * t, 128, 0)]
        else:
            left = [(0, 0, 128 * t, 0), (128 * t + 128, 128 * t + 128, 896 - 128 * t, 1)]
        for col, key, n, side in left:
            a, z = max(col, c0), min(col + n, c1)
            if z > a:
                out.append((a, key + a - col, z - a, side))
        return out

    def s_pass(g):
        z = g % 2
        for hh in range(4):
            n = 4 * g + hh
            s = n % NS
            for t in range(8):
                slot = sdlist.pop(0)
                sdslot[(n, t)] = slot
                for u in range(2):
                    def fill(bank, free):
                        for col, key, ln, side in pieces(t, 512 * u, 512 * u + 512, True):
                            tok = c.mm(bank[:, col - 512 * u:col - 512 * u + ln],
                                       qst[0:96, s, side, 128 * t:128 * t + 128],
                                       kst[0:96, s, 1 - side, key:key + ln], filled[n], free)
                        return tok

                    def use(bank, tok):
                        if u == 0:
                            return dve.do(lambda e, hh=hh, t=t: e.tensor_reduce(
                                mx[:, z, hh, t, 0:1], bank[:, 0:512], op=ALU.max, axis=AX.X), tok, mdone.get(g - 2))
                        dve.do(lambda e, hh=hh, t=t: e.tensor_reduce(
                            mx[:, z, hh, t, 1:2], bank[:, 0:384], op=ALU.max, axis=AX.X), tok, mdone.get(g - 2))
                        sdtok[(n, t)] = dve.do(lambda e, hh=hh, t=t, slot=slot: e.tensor_tensor_reduce(
                            out=Sd[:, slot, :], in0=bank[:, 384:512], in1=Dm[:], scale=1.0, scalar=-3.0e38,
                            op0=ALU.mult, op1=ALU.max, accum_out=mx[:, z, hh, t, 2:3]), tok, sdfree[slot], loaded)
                        return sdtok[(n, t)]
                    c.unit(fill, use)
                    yield
        mdone[g] = dve.do(lambda e: e.tensor_reduce(m[:, z, :], mx[:, z].rearrange("p h t k -> p (h t) k"),
                                                   op=ALU.max, axis=AX.X), dve.last(), sdtok.get(("mfree", g - 2)))
        for hh in range(4):
            for t in range(8):
                n = 4 * g + hh
                slot = sdslot[(n, t)]
                i = 8 * hh + t
                sdtok[(n, t)] = pool.do(lambda e, slot=slot, i=i: e.tensor_tensor(
                    Sd[:, slot, :], Sd[:, slot, :], m[:, z, i:i + 1].to_broadcast([128, 128]), ALU.subtract), mdone[g])
        sdtok[("mfree", g)] = sdtok[(n, 7)]

        def fill(bank, free):
            return c.tr(bank[0:32, 0:128], m[:, z, :], ident[:], mdone[g], free)

        def use(bank, tok):
            return dve.do(lambda e: e.tensor_scalar_mul(mT[:], bank[0:32, 0:128], -1.0), tok, pool.last())
        mtr = {}

        def fill2(bank, free):
            mtr[0] = fill(bank, free)
            return mtr[0]
        c.unit(fill2, use)
        yield
        t0 = dve.last()
        t1 = dve.do(lambda e: e.tensor_copy(mp[:, 0, :], mT[:]), t0, s_m.last())
        t2 = dve.do(lambda e: e.tensor_tensor(mTr[:], mT[:], mp[:, 0, :], ALU.subtract), t1)
        t3 = dve.do(lambda e: e.tensor_copy(mp[:, 1, :], mTr[:]), t2)
        t4 = dve.do(lambda e: e.tensor_tensor(mp[:, 2, :], mTr[:], mp[:, 1, :], ALU.subtract), t3)
        sdtok[("mfree", g)] = sdtok[("mfree", g)]
        wr = sp.dma(s_m, mdram[z].rearrange("c h t -> h c t").rearrange("h c (t q) -> (h t) c q", q=128)
                    if False else mdram[z], mp[:], t4, mrow.get(("r", g - 2)))
        for hh in range(4):
            n = 4 * g + hh
            s = n % NS
            for v in range(2):
                mrow[n] = sp.dma(s_mr[s], qst[96:99, s, v, :].rearrange("c (t q) -> c t q", q=128),
                                 mdram[z, 8 * hh:8 * hh + 8].rearrange("t c q -> c t q"), wr,
                                 tdone.get((n - NS) // 4) if n >= NS else None)
                for_r = mrow[n]
            mrow[("r", g)] = for_r
        mrow[("all", g)] = [mrow[4 * g + hh] for hh in range(4)]

    pfree = [None] * NP
    pn = [0]
    tfree = [None, None]
    tn = [0]
    pvfree = [v0]

    def t_pass(g):
        b = g // 4
        pv = []
        for kb in range(8):
            bufs = []
            for hh in range(4):
                n = 4 * g + hh
                s = n % NS
                i = tn[0] % 2
                tn[0] += 1
                bank = c.T[i]
                for u in range(2):
                    for col, q0, ln, side in pieces(kb, 512 * u, 512 * u + 512, False):
                        c.mm(bank[:, col:col + ln], kst[0:99, s, side, 128 * kb:128 * kb + 128],
                             qst[0:99, s, 1 - side, q0:q0 + ln], filled[n], mrow[n], ones_k, tfree[i])
                slot = sdslot[(n, kb)]
                tok = c.tr(bank[:, 128 * kb:128 * kb + 128], Sd[:, slot, :], ident[:], sdtok[(n, kb)], tfree[i])
                sdfree[slot] = tok
                sdlist.append(slot)
                pi = pn[0] % NP
                pn[0] += 1
                ex = act.do(lambda e, pi=pi, bank=bank: e.activation(P[:, pi, :], bank, ACT.Exp), tok, pfree[pi])
                tfree[i] = ex
                bufs.append((pi, ex))
                yield
                if len(pv) == 4 and hh == 1:
                    emit_pv(g, b, kb - 1, pv)
                    pv = []
            pv = bufs
        tdone[g] = pe.last()
        emit_pv(g, b, 7, pv)
        pd = pe.last()
        vread[b] = pd
        ev = act.do(lambda e: e.activation(Ou[:], c.V, ACT.Copy), pd, wfold["o"])
        pvfree[0] = ev
        yield
        for ch in range(2):
            def fill(bank, free):
                for t in range(4):
                    tok = c.tr(bank[:, 128 * t:128 * t + 128], Ou[:, 512 * ch + 128 * t:512 * ch + 128 * t + 128],
                               ident[:], ev, free)
                wfold["o"] = tok
                return tok

            def use(bank, tok):
                v4 = bank[:].rearrange("p (t h x) -> p t h x", t=4, h=4)
                r1 = dve.do(lambda e, v4=v4: e.reciprocal(rc[:], v4[:, :, :, 16]), tok, dve.last())
                g4 = 64 * (g % 4)
                return dve.do(lambda e, v4=v4, ch=ch, g4=g4: e.tensor_tensor(
                    OT[:, 4 * ch:4 * ch + 4, g4:g4 + 64].rearrange("p t (h x) -> p t h x", h=4),
                    v4[:, :, :, 0:16], rc[:].rearrange("p t (h o) -> p t h o", o=1).to_broadcast([128, 4, 4, 16]),
                    ALU.mult), r1, wfold.get("otr"))
            c.unit(fill, use)
            yield
        if g % 4 == 3:
            otd = dve.last()
            for ch in range(2):
                ofd = None
                for k in range(2):
                    def fill(bank, free):
                        for t in range(4):
                            tok = c.tr(bank[:, 128 * t:128 * t + 128], OT[:, 4 * ch + t, 128 * k:128 * k + 128],
                                       ident[:], otd, free)
                        wfold["otr"] = tok
                        return tok

                    def use(bank, tok):
                        wfold["of"] = act.do(lambda e, k=k: e.activation(OF[:, k, :], bank[:], ACT.Copy), tok, wfold.get("pj"))
                        return wfold["of"]
                    c.unit(fill, use)
                    yield
                for t in range(4):
                    tt = 4 * ch + t
                    r = tt % 2
                    ld = sp.dma(s_res[r], res[:, r, :], x1[b, 128 * tt:128 * tt + 128, :], s_yr[r].last())

                    def fill(bank, free):
                        for k in range(2):
                            tok = c.mm(bank[:, 0:D], OF[:, k, 128 * t:128 * t + 128], wo[:, k, :], wfold["of"], free,
                                       start=(k == 0), stop=(k == 1))
                        wfold["pj"] = tok
                        return tok

                    def use(bank, tok):
                        rr = dve.do(lambda e, r=r: e.tensor_tensor(res[:, r, :], bank[:, 0:D], res[:, r, :], ALU.add), tok, ld)
                        sp.dma(s_yr[r], x2[b, 128 * tt:128 * tt + 128, :], res[:, r, :], rr)
                        return rr
                    c.unit(fill, use)
                    yield

    wfold = {"o": setup}

    def emit_pv(g, b, kb, pv):
        for ch in range(2):
            for hh in range(4):
                pi, ex = pv[hh]
                h = (4 * g + hh) % H
                tok = c.mm(c.V[32 * hh:32 * hh + 17, 512 * ch:512 * ch + 512], V[:, b % 2, kb, h, :],
                           P[:, pi, 512 * ch:512 * ch + 512], ex, vdone[b], ones_v, pvfree[0],
                           start=(kb == 0), stop=(kb == 7))
                if ch == 1:
                    pfree[pi] = tok

    for _ in prep(0):
        pass
    for n in range(min(NS, 8)):
        fill_stack(n)
    nfill = min(NS, 8)
    for _ in s_pass(0):
        pass
    NG = NH // 4
    gp = None
    for g in range(NG):
        tp = t_pass(g)
        spass = s_pass(g + 1) if g + 1 < NG else iter(())
        if g % 4 == 0:
            gp = prep(g // 4 + 1) if g // 4 + 1 < B else iter(())
        lim = min(NH, 4 * g + NS)
        step = 0
        for _ in tp:
            while nfill < lim and nfill // H in pdone:
                fill_stack(nfill)
                nfill += 1
            next(spass, None)
            next(spass, None)
            next(gp, None)
            step += 1
        for _ in spass:
            pass
        if g % 4 == 2:
            for _ in gp:
                pass
        while nfill < lim and nfill // H in pdone:
            fill_stack(nfill)
            nfill += 1
    ctx.close()
    return [s.last() for s in s_yr]


def consts():
    t = np.arange(S, dtype=np.float64) - (S / 2 - 0.5)
    i = np.arange(128, dtype=np.float64)
    e = np.arange(E, dtype=np.float32)
    misc = np.concatenate([np.tile(e, (128, 1)), np.tile(e * CAP, (128, 1)), i[:, None]], 1).astype(np.float32)
    return {
        "tri": (i[:, None] < i[None, :]).astype(np.float32),
        "misc": misc,
        "jf": np.arange(NBLK, dtype=np.float32)[None, :],
        "ident": np.eye(128, dtype=np.float32),
        "decn": np.tile(np.exp(-LAM * t).astype(np.float32), (128, 1)),
        "decp": np.tile(np.exp(LAM * t).astype(np.float32), (128, 1)),
        "dm": np.exp(np.minimum(0.0, 2 * LAM * (i[:, None] - i[None, :]))).astype(np.float32),
    }


_INS = ['L0_attn_x', 'L0_attn_W_q', 'L0_attn_W_k', 'L0_attn_W_v', 'L0_attn_W_o', 'L0_attn_W_down_kv', 'L0_attn_W_up_k',
        'L0_attn_W_up_v', 'L0_ffn_router_w', 'L0_ffn_router_b', 'L0_ffn_we_gate', 'L0_ffn_we_up', 'L0_ffn_we_down']
_ROUTE = ("ident", "tri", "misc", "jf")


def program(nc, a, cst, out):
    B = 16
    x, wq, wk, wv, wo, wdn, wuk, wuv, rw, rb, eg, eu, ed = a
    with ExitStack() as ctx:
        c = Core(nc, ctx)
        x1 = nc.dram_tensor("x1", [B, S, D], F32).ap()
        x2 = nc.dram_tensor("x2", [B, S, D], F32).ap()
        xs = nc.dram_tensor("xs", [E * CAP, D], F32).ap()
        ys = nc.dram_tensor("ys", [NBLK * 128, D], F32).ap()
        parts = nc.dram_tensor("parts", [2, 2, H, 3, HD, 2, S], BF16).ap()
        mdram = nc.dram_tensor("mdram", [2, 32, 3, 128], BF16).ap()
        we = {"rw": rw, "rb": rb, "g": eg, "u": eu, "d": ed}
        wa = {"q": wq, "k": wk, "v": wv, "o": wo, "down": wdn, "upk": wuk, "upv": wuv}

        def flat(t):
            return t.rearrange("b s d -> (b s) d")
        moe(c, B * S // 128, flat(x), flat(x1), xs, ys, cst, we, [], "m1")
        c.meet()
        attention(c, B, x1, x2, parts, mdram, cst, wa)
        c.meet()
        moe(c, B * S // 128, flat(x2), flat(out), xs, ys, cst, we, [], "m2")
        ends = [s.last() for s in c.streams if s.n]
        block = ctx.enter_context(nc.Block())

        @block.sync
        def _(e):
            c.sp.run(e)
            for sem, n, _k in ends:
                e.wait_ge(sem, n)

        @block.scalar
        def _(e):
            c.act.run(e)

        @block.vector
        def _(e):
            c.dve.run(e)

        @block.tensor
        def _(e):
            c.pe.run(e)

        @block.gpsimd
        def _(e):
            c.pool.run(e)


def kernel(**inputs):
    import concourse.bacc as _bacc
    from concourse.bass_utils import run_bass_kernel_spmd as _run

    nc = _bacc.Bacc("TRN2", target_bir_lowering=False, num_devices=1)
    arrays, args = {}, []
    for name in _INS:
        v = np.ascontiguousarray(inputs[name])
        arrays[f"in_{name}"] = v
        args.append(nc.dram_tensor(f"in_{name}", v.shape, mybir.dt.from_np(v.dtype), kind="ExternalInput").ap())
    cst = {}
    for name, v in consts().items():
        arrays[f"const_{name}"] = v
        cst[name] = nc.dram_tensor(f"const_{name}", v.shape, F32, kind="ExternalInput").ap()
    out = nc.dram_tensor("out", (16, S, D), F32, kind="ExternalOutput").ap()
    program(nc, args, cst, out.rearrange("b s d -> b s d"))
    r = _run(nc, [arrays], core_ids=[0])
    return r.results[0]["out"]
```

```python
import concourse.bass as bass
from concourse import mybir
from contextlib import ExitStack
import numpy as np

F32 = mybir.dt.float32
BF16 = mybir.dt.bfloat16
F32R = mybir.dt.float32r
I32 = mybir.dt.int32
U32 = mybir.dt.uint32
ACT = mybir.ActivationFunctionType
ALU = mybir.AluOpType
AX = mybir.AxisListType

D = 256
S = 1024
H = 16
HD = 16
DL = 64
E = 8
LAM = 0.01
EPS = 1e-5
NS = 10
FAR = (float(np.exp(LAM * S / 4)), float(np.exp(-LAM * S / 4)))
NP = 12
NR = 3


class Queue:

    def __init__(self, sem):
        self.sem, self.n, self.items, self.seen, self.hold = sem, 0, [], {}, []

    def do(self, f, *after, mark=True):
        waits = []
        after, self.hold = [*self.hold, *after], []
        for tok in after:
            if tok is None:
                continue
            s, v, key = tok
            if self.seen.get(key, 0) < v:
                self.seen[key] = v
                waits.append((s, v))
        tok = None
        if mark:
            self.n += 1
            tok = (self.sem, self.n, id(self.sem))
        self.items.append((waits, f, (self.sem, 1) if mark else None))
        return tok

    def dma(self, stream, out, in_, *after):
        self.do(lambda e: e.dma_start(out, in_), *after, mark=False)
        waits, f, _ = self.items[-1]
        self.items[-1] = (waits, f, (stream.sem, 16))
        return stream.count()

    def last(self):
        return (self.sem, self.n, id(self.sem)) if self.n else None

    def run(self, eng):
        for waits, f, inc in self.items:
            for s, v in waits:
                eng.wait_ge(s, v)
            ins = f(eng)
            if inc:
                ins.then_inc(*inc)


class Stream:

    def __init__(self, sem):
        self.sem, self.n = sem, 0

    def count(self):
        self.n += 16
        return self.last()

    def last(self):
        return (self.sem, self.n, id(self.sem)) if self.n else None


class Core:

    def __init__(self, nc, ctx):
        self.nc, self.ctx, self.streams = nc, ctx, []
        self.pe, self.dve, self.act, self.pool, self.sp = (
            Queue(self.sem(n)) for n in ("s_pe", "s_dve", "s_act", "s_pool", "s_sp"))
        ps = ctx.enter_context(nc.psum_tensor("psum", [128, 4096], F32))
        self.bank = [ps[:, 512 * i:512 * i + 512] for i in range(8)]
        self.A = self.bank[0:4]
        self.T = self.bank[4:7]
        self.V = self.bank[7]
        self.a_n = 0
        self.a_free = [None] * len(self.A)

    def sem(self, name):
        return self.ctx.enter_context(self.nc.semaphore(name))

    def stream(self, name):
        self.streams.append(Stream(self.sem(name)))
        return self.streams[-1]

    def unit(self, fill, use):
        i = self.a_n % len(self.A)
        self.a_n += 1
        tok = fill(self.A[i], self.a_free[i])
        self.a_free[i] = use(self.A[i], tok)

    def meet(self):
        at = [q.last() for q in (self.pe, self.dve, self.act, self.pool, self.sp)]
        at += [s.last() for s in self.streams]
        for q in (self.pe, self.dve, self.act, self.pool, self.sp):
            q.hold = at

    def mm(self, out, lhsT, rhs, *after, start=True, stop=True, mark=True):
        return self.pe.do(lambda e: e.matmul(out, lhsT, rhs, start=start, stop=stop), *after, mark=mark)

    def tr(self, out, in_, ident, *after, mark=True):
        return self.pe.do(lambda e: e.transpose(out, in_, ident), *after, mark=mark)


CAP = 16512
CB = CAP // 128
NBLK = 264
HALVES = ((0, 0), (0, 1), (1, 0)) * 2


class Ring:

    def __init__(self, banks):
        self.banks, self.n, self.free = banks, 0, [None] * len(banks)

    def take(self):
        i = self.n % len(self.banks)
        self.n += 1
        return i, self.banks[i], self.free[i]


def moe(c, NT, xin, out, xs, ys, cst, w, begin, tag):
    nc, pe, dve, act, pool, sp = c.nc, c.pe, c.dve, c.act, c.pool, c.sp
    ctx = ExitStack()

    def sb(name, shape, dt=F32):
        return ctx.enter_context(nc.sbuf_tensor(tag + name, shape, dt))

    wgu = [sb(f"wgu{i}", [128, 2, E * 512], F32R) for i in range(2)]
    wdn = [sb(f"wdn{i}", [128, 2, E * D], F32R) for i in range(2)]
    wst = sb("wst", [128, 2, 2, D])
    rw = sb("rw", [128, 2, E])
    rb = sb("rb", [128, E])
    ident = sb("ident", [128, 128])
    tri = sb("tri", [128, 128], BF16)
    ones = sb("ones", [128, 128], BF16)
    trif = sb("trif", [128, 128])
    misc = sb("misc", [128, 8 + 8 + 1])
    iota8, ecap, iotap = misc[:, 0:8], misc[:, 8:16], misc[:, 16:17]
    jf = sb("jf", [1, NBLK])
    zero = sb("zero", [128, D])
    P = sb("P", [128, NT, 2])
    EX = sb("EX", [128, NT, 2])
    M = sb("M", [128, NT, 2])
    XB, Z = 8, 4
    X = sb("X", [128, XB, 4, D])
    xT = sb("xT", [128, Z, 2, 512])
    st = sb("st", [128, Z, 4, 6])
    mv = sb("mv", [128, Z, 4, 2])
    ve = sb("ve", [128, Z, 4])
    sq = sb("sq", [128, Z, 4])
    rs = sb("rs", [128, Z, 4])
    lg = sb("lg", [128, Z, 4, E])
    m8 = sb("m8", [128, Z, 4, 8])
    i8 = sb("i8", [128, Z, 4, 8], U32)
    OH = sb("OH", [128, Z, 4, 2, E])
    O = sb("O", [128, Z, 4, E], BF16)
    base = sb("base", [128, 2, E])
    rk = sb("rk", [128, Z, 4, E])
    pr = sb("pr", [128, Z, 4, 2, E])
    idx = sb("idx", [128, XB, 4, 2], U32)
    s_w, s_pad = (c.stream(tag + n) for n in ("w", "pad"))
    s_ld = [c.stream(f"{tag}ld{i}") for i in range(XB)]
    s_sc = [c.stream(f"{tag}sc{i}") for i in range(XB)]

    def dv(f, *after):
        return dve.do(f, *after)

    ldc = None
    for dst, src in ((ident[:], cst["ident"]), (trif[:], cst["tri"]), (misc[:], cst["misc"]), (jf[:], cst["jf"]),
                     (rw[:], w["rw"].rearrange("(k p) n -> p k n", p=128)),
                     (rb[:], w["rb"].rearrange("(o n) -> o n", o=1).to_broadcast([128, E]))):
        ldc = sp.dma(s_w, dst, src, *begin)
    k1 = dv(lambda e: e.tensor_copy(tri[:], trif[:]), ldc)
    k2 = dv(lambda e: e.memset(ones[:], 1.0))
    k3 = dv(lambda e: e.memset(zero[:], 0.0))
    bt = dv(lambda e: e.tensor_copy(base[:, 0, :], ecap), ldc)
    setup = bt

    xv = xin.rearrange("(g t p) d -> g p t d", p=128, t=4)
    ov = out.rearrange("(g t p) d -> g p t d", p=128, t=4)
    NG = NT // 4
    ring = Ring(c.bank)
    okd = {}
    scat = {}
    loads = {}

    def load(g):
        loads[g] = sp.dma(s_ld[g % XB], X[:, g % XB], xv[g], scat.get(g - XB))
    for g in range(min(XB, NG)):
        load(g)
    tb = {}
    bts = [bt]

    def route(g):
        z, xb = g % Z, g % XB
        zb = g % 2
        pz = tb.get(g - Z)
        for t in range(4):
            a = dv(lambda e, t=t, z=z, xb=xb: e.bn_stats(st[:, z, t, :], X[:, xb, t, :]), loads[g], pz)
        for t in range(4):
            a2 = dv(lambda e, t=t, z=z: e.bn_aggr(mv[:, z, t, :], st[:, z, t, :]), a)
        a = dv(lambda e, z=z: e.tensor_scalar_add(ve[:, z, :], mv[:, z, :, 1], EPS), a2)
        yield
        q = act.do(lambda e, z=z: e.activation(sq[:, z, :], ve[:, z, :], ACT.Sqrt), a, pz)
        yield
        a = dv(lambda e, z=z: e.reciprocal(rs[:, z, :], sq[:, z, :]), q)
        a = dv(lambda e, z=z: e.tensor_tensor(sq[:, z, :], rs[:, z, :], rs[:, z, :], ALU.mult), a)
        a = dv(lambda e, z=z: e.tensor_tensor(sq[:, z, :], sq[:, z, :], ve[:, z, :], ALU.mult), a)
        a = dv(lambda e, z=z: e.tensor_scalar(sq[:, z, :], sq[:, z, :], -0.5, 1.5, ALU.mult, ALU.add), a)
        a = dv(lambda e, z=z: e.tensor_tensor(rs[:, z, :], rs[:, z, :], sq[:, z, :], ALU.mult), a)
        for t in range(4):
            xn = dv(lambda e, t=t, z=z, xb=xb: e.tensor_scalar(X[:, xb, t, :], X[:, xb, t, :], mv[:, z, t, 0:1],
                                                             rs[:, z, t:t + 1], ALU.subtract, ALU.mult), a)
        yield
        for k in range(2):
            i, bank, free = ring.take()
            for t in range(4):
                tok = c.tr(bank[:, 128 * t:128 * t + 128], X[:, xb, t, 128 * k:128 * k + 128], ident[:], xn, free, ldc)
            ring.free[i] = act.do(lambda e, k=k, z=z, bank=bank: e.activation(xT[:, z, k, :], bank, ACT.Copy),
                                  tok, okd.get(g - Z))
        xtd = ring.free[i]
        yield
        i, bank, free = ring.take()
        for t in range(4):
            for k in range(2):
                tok = c.mm(bank[:, E * t:E * t + E], xT[:, z, k, 128 * t:128 * t + 128], rw[:, k, :], xtd, free,
                           start=(k == 0), stop=(k == 1))
        okd[g] = tok
        yield
        a = ring.free[i] = dv(lambda e, z=z, bank=bank: e.tensor_tensor(
            lg[:, z], bank[:, 0:32].rearrange("p (t e) -> p t e", t=4),
            rb[:].rearrange("p (o e) -> p o e", o=1).to_broadcast([128, 4, E]), ALU.add), tok)
        for t in range(4):
            b1 = dv(lambda e, t=t, z=z: e.max(m8[:, z, t, :], lg[:, z, t, :]), a)
        for t in range(4):
            b2 = dv(lambda e, t=t, z=z: e.max_index(i8[:, z, t, :], m8[:, z, t, :], lg[:, z, t, :]), b1)
        dv(lambda e, z=z, g=g: e.tensor_copy(M[:, 4 * g:4 * g + 4, :], m8[:, z, :, 0:2]), b1)
        b3 = dv(lambda e, z=z, g=g: e.tensor_copy(EX[:, 4 * g:4 * g + 4, :], i8[:, z, :, 0:2]), b2)
        b4 = dv(lambda e, z=z, g=g: e.tensor_tensor(
            OH[:, z], EX[:, 4 * g:4 * g + 4, :].rearrange("p t (k o) -> p t k o", o=1).to_broadcast([128, 4, 2, E]),
            iota8.rearrange("p (a b e) -> p a b e", a=1, b=1).to_broadcast([128, 4, 2, E]), ALU.is_equal), b3)
        b5 = dv(lambda e, z=z: e.tensor_tensor(O[:, z], OH[:, z, :, 0, :], OH[:, z, :, 1, :], ALU.add), b4, tb.get(("pe", g - Z)))
        yield
        i, bank, free = ring.take()
        r4 = bank[:, 0:32].rearrange("p (t e) -> p t e", t=4)
        c.mm(r4, tri[:], O[:, z], b5, free, k1, k2, start=True, stop=False)
        for t in range(3):
            c.mm(r4[:, t + 1:4, :], ones[:], O[:, z, t:t + 1, :].to_broadcast([128, 3 - t, E]), start=False, stop=(t == 2))
        for t in range(4):
            tok = c.mm(bank[:, 32:40], ones[:], O[:, z, t, :], start=(t == 0), stop=(t == 3))
        tb[("pe", g)] = tok
        yield
        b6 = dv(lambda e, z=z, zb=zb, r4=r4: e.tensor_tensor(
            rk[:, z], r4, base[:, zb].rearrange("p (o e) -> p o e", o=1).to_broadcast([128, 4, E]), ALU.add), tok, bts[0])
        bts[0] = ring.free[i] = dv(lambda e, zb=zb, bank=bank: e.tensor_tensor(base[:, 1 - zb], base[:, zb], bank[:, 32:40], ALU.add),
                               b6)
        b7 = dv(lambda e, z=z: e.tensor_tensor(
            pr[:, z], OH[:, z], rk[:, z].rearrange("p t (o e) -> p t o e", o=1).to_broadcast([128, 4, 2, E]), ALU.mult), b6)
        b8 = dv(lambda e, z=z, g=g: e.tensor_reduce(P[:, 4 * g:4 * g + 4, :], pr[:, z], op=ALU.add, axis=AX.X), b7)
        b9 = dv(lambda e, g=g, xb=xb: e.tensor_copy(idx[:, xb], P[:, 4 * g:4 * g + 4, :]), b8, scat.get(g - XB))
        tb[g] = b9
        for t in range(4):
            for k in range(2):
                pool.do(lambda e, t=t, k=k, xb=xb: e.indirect_dma_start(
                    xs, bass.IndirectOffsetOnAxis(ap=idx[:, xb, t, k:k + 1], axis=0), X[:, xb, t, :], None),
                    b9, k3, *(begin if g == 0 else ()), mark=False)
                wts, f, _ = pool.items[-1]
                pool.items[-1] = (wts, f, (s_sc[xb].sem, 16))
                scat[g] = s_sc[xb].count()

    s_ws = [c.stream(f"{tag}ws{i}") for i in range(2)]
    wfree = [None, None]
    wl = None

    def high(i, ld, dst):
        return act.do(lambda e: e.activation(dst[0], wst[:, i], ACT.Copy), ld)

    def low(i, hi, dst):
        lo = dv(lambda e: e.tensor_tensor(dst[1], wst[:, i], dst[0].bitcast(F32), ALU.subtract), hi)
        wfree[i] = lo
        return lo

    shares, wlow = [], []
    for x in range(E):
        for h in range(2):
            shares.append((w["gu"[h]][x], [t[:].rearrange("p k (e h n) -> p k e h n", e=E, h=2)[:, :, x, h, :] for t in wgu]))
        shares.append((w["d"][x], [t[:].rearrange("p k (e n) -> p k e n", e=E)[:, :, x, :] for t in wdn]))

    def weights():
        def fetch(i):
            return sp.dma(s_ws[i % 2], wst[:, i % 2], shares[i][0].rearrange("(k p) n -> p k n", p=128), wfree[i % 2], *begin)
        nxt = fetch(0)
        for i, (_s, dst) in enumerate(shares):
            ld, nxt = nxt, None
            if wlow:
                wlow.pop()()
            if i + 1 < len(shares):
                nxt = fetch(i + 1)
            hi = high(i % 2, ld, dst)
            wlow.append(lambda i=i, hi=hi, dst=dst: low(i % 2, hi, dst))
            yield
        wlow.pop()()
    wgen = weights()
    live = {}
    for g in range(NG + 4):
        while len(loads) < NG and len(loads) - XB in scat:
            load(len(loads))
        if g < NG:
            live[g] = route(g)
        for back, steps in ((4, 1), (2, 2), (3, 2), (1, 1), (0, 2)):
            if 0 <= g - back < NG:
                for _s in range(steps):
                    next(live[g - back], None)
        next(wgen, None)
    for _s in wgen:
        pass
    wl = dve.last()
    bt = bts[0]
    zf = NG % 2
    cnt = sb("cnt", [128, E])
    nbi = sb("nbi", [128, E], I32)
    nb = sb("nb", [128, E])
    bend = sb("bend", [128, E])
    ysh = sb("ysh", [128, E])
    dl = sb("dl", [128, E])
    tot = sb("tot", [128, 1])
    padf = sb("padf", [128, E])
    padi = sb("padi", [128, E], U32)
    jt = sb("jt", [1, 4, NBLK])
    tabE = sb("tabE", [1, NBLK], I32)
    tabR = sb("tabR", [1, NBLK], I32)
    G = sb("G", [128, NT, 2])
    T1 = sb("T1", [128, NT, 2])
    yi = sb("yi", [128, NT, 2], U32)
    a = dv(lambda e: e.tensor_scalar(padf[:], base[:, zf], iotap, None, ALU.add), bt)
    padr = dv(lambda e: e.tensor_copy(padi[:], padf[:]), a)
    for x in range(E):
        pool.do(lambda e, x=x: e.indirect_dma_start(
            xs, bass.IndirectOffsetOnAxis(ap=padi[:, x:x + 1], axis=0), zero[:], None), padr, mark=False)
        wts, f, _ = pool.items[-1]
        pool.items[-1] = (wts, f, (s_pad.sem, 16))
        pads = s_pad.count()
    scattered = [s.last() for s in s_sc] + [pads]
    a = dv(lambda e: e.tensor_tensor(cnt[:], base[:, zf], ecap, ALU.subtract), bt)
    a = dv(lambda e: e.tensor_scalar_add(cnt[:], cnt[:], 127.0), a)
    a = dv(lambda e: e.tensor_copy(nbi[:], cnt[:]), a)
    a = dv(lambda e: e.tensor_single_scalar(nbi[:], nbi[:], 7, ALU.arith_shift_right), a)
    a = dv(lambda e: e.tensor_copy(nb[:], nbi[:]), a)
    a = dv(lambda e: e.tensor_copy(bend[:, 0:1], nb[:, 0:1]), a)
    for x in range(1, E):
        a = dv(lambda e, x=x: e.tensor_tensor(bend[:, x:x + 1], bend[:, x - 1:x], nb[:, x:x + 1], ALU.add), a)
    dv(lambda e: e.tensor_scalar_add(tot[:], bend[:, E - 1:E], -1.0), a)
    a = dv(lambda e: e.tensor_tensor(ysh[:], bend[:], nb[:], ALU.subtract), a)
    a = dv(lambda e: e.tensor_scalar_mul(ysh[:], ysh[:], 128.0), a)
    a = dv(lambda e: e.tensor_tensor(ysh[:], ysh[:], ecap, ALU.subtract), a)
    a = dv(lambda e: e.tensor_scalar(dl[:], nb[:], -1.0, float(CB), ALU.mult, ALU.add), a)
    a = dv(lambda e: e.tensor_scalar(jt[:, 0], jf[:], tot[0:1, :], None, ALU.min), a)
    dv(lambda e: e.tensor_copy(jt[:, 2], jt[:, 0]), a)
    a = dv(lambda e: e.memset(jt[:, 1], 0.0))
    for x in range(E - 1):
        a = dv(lambda e, x=x: e.tensor_scalar(jt[:, 3], jt[:, 0], bend[0:1, x:x + 1], None, ALU.is_ge), a)
        dv(lambda e: e.tensor_tensor(jt[:, 1], jt[:, 1], jt[:, 3], ALU.add), a)
        a = dv(lambda e, x=x: e.scalar_tensor_tensor(jt[:, 2], jt[:, 3], dl[0:1, x:x + 1], jt[:, 2], ALU.mult, ALU.add), a)
        a = dve.last()
    dv(lambda e: e.tensor_scalar_mul(jt[:, 3], jt[:, 2], 1.0), a)
    a = dve.last()
    dv(lambda e: e.tensor_copy(tabE[:], jt[:, 1]), a)
    tabs = dv(lambda e: e.tensor_copy(tabR[:], jt[:, 3]), a)
    after = {}

    def results():
        a = tabs
        for x in range(E):
            a = dv(lambda e, x=x: e.tensor_scalar(T1[:], EX[:], float(x), ysh[:, x:x + 1], ALU.is_equal, ALU.mult), a, dve.last())
            a = dv(lambda e: e.tensor_tensor(P[:], P[:], T1[:], ALU.add), a)
        rows = dv(lambda e: e.tensor_copy(yi[:], P[:]), a)
        a = dv(lambda e: e.tensor_tensor(G[:, :, 1], M[:, :, 1], M[:, :, 0], ALU.subtract), a)
        a = act.do(lambda e: e.activation(G[:, :, 1], G[:, :, 1], ACT.Exp), a)
        a = dv(lambda e: e.tensor_scalar(T1[:, :, 0], G[:, :, 1], 2.0, 2.0, ALU.mult, ALU.add), a, rows)
        a = dv(lambda e: e.reciprocal(G[:, :, 0], T1[:, :, 0]), a)
        gates = dv(lambda e: e.tensor_tensor(G[:, :, 1], G[:, :, 1], G[:, :, 0], ALU.mult), a)
        after["rows"], after["gates"] = rows, gates

    NX, NYB = 8, 6
    xb_ = X[:].rearrange("p a b d -> p (a b) d")
    xg, yb, sg, hb = xb_[:, 0:NX], xb_[:, NX:NX + NYB], xb_[:, 14:16], xb_[:, 16:18]
    xgT = sb("xgT", [128, 3, 2, 256], F32R)
    hT = sb("hT", [128, 2, 2, 256], F32R)
    s_xg = [c.stream(f"{tag}xg{i}") for i in range(NX)]
    s_yo = [c.stream(f"{tag}yo{i}") for i in range(NYB)]
    bk = c.bank
    tx = Ring([bk[0], bk[1]])
    gu = Ring([bk[2], bk[3]])
    th = Ring([bk[4], bk[5]])
    yk = Ring([bk[6], bk[7]])
    rE, rR = {}, {}
    n_tr = {}
    xl, xtd, gud, htd, hd, trh = {}, {}, {}, {}, {}, {}
    dwn = {}
    ydone = {}
    pe_regs = {}
    quiet = [tabs, act.last(), pe.last(), *scattered]

    def xload(j):
        def f(e):
            r = e.value_load(tabR[0:1, j:j + 1], min_val=0, max_val=8 * CB - 1)
            return e.dma_start(xg[:, j % NX], xs[bass.ds(r * 128, 128), :])
        sp.do(f, tabs, *quiet, n_tr.get(j - NX), mark=False)
        wts, f, _ = sp.items[-1]
        sp.items[-1] = (wts, f, (s_xg[j % NX].sem, 16))
        xl[j] = s_xg[j % NX].count()

    def trx(j):
        i, bank, free = tx.take()
        for k in range(2):
            tok = c.tr(bank[:, 128 * k:128 * k + 128], xg[:, j % NX, 128 * k:128 * k + 128], ident[:], xl[j], free, *quiet)
        n_tr[j] = tok
        hi = act.do(lambda e: e.activation(xgT[:, j % 3, 0], bank[:, 0:256], ACT.Copy), tok, gud.get(j - 3))
        tx.free[i] = xtd[j] = dv(lambda e: e.tensor_tensor(
            xgT[:, j % 3, 1], bank[:, 0:256], xgT[:, j % 3, 0].bitcast(F32), ALU.subtract), hi, gud.get(j - 3))

    def gate_up(j):
        def f(e):
            r = e.value_load(tabE[0:1, j:j + 1], min_val=0, max_val=E - 1)
            rE[j] = r
            return None
        pe.do(f, tabs, mark=False)
        i, bank, free = gu.take()
        for k, (p, q) in enumerate(HALVES):
            tok = pe.do(lambda e, k=k, p=p, q=q, bank=bank: e.matmul(
                bank, xgT[:, j % 3, p, 128 * (k // 3):128 * (k // 3) + 128], wgu[q][:, k // 3, bass.ds(rE[j] * 512, 512)],
                start=(k == 0), stop=(k == 5)), xtd[j], free, wl)
        gud[j] = tok
        a = act.do(lambda e: e.activation(sg[:, j % 2], bank[:, 0:256], ACT.Silu), tok, hd.get(j - 2), quiet[2])
        hd[j] = gu.free[i] = dv(lambda e: e.tensor_tensor(hb[:, j % 2], sg[:, j % 2], bank[:, 256:512], ALU.mult), a,
                                trh.get(j - 2))

    def trh_(j):
        i, bank, free = th.take()
        for k in range(2):
            tok = c.tr(bank[:, 128 * k:128 * k + 128], hb[:, j % 2, 128 * k:128 * k + 128], ident[:], hd[j], free)
        trh[j] = tok
        hi = dv(lambda e: e.tensor_copy(hT[:, j % 2, 0], bank[:, 0:256]), tok, dwn.get(j - 2))
        th.free[i] = htd[j] = dv(lambda e: e.tensor_tensor(
            hT[:, j % 2, 1], bank[:, 0:256], hT[:, j % 2, 0].bitcast(F32), ALU.subtract), hi)

    def down(j):
        i, bank, free = yk.take()
        for k, (p, q) in enumerate(HALVES):
            tok = pe.do(lambda e, k=k, p=p, q=q, bank=bank: e.matmul(
                bank[:, 0:D], hT[:, j % 2, p, 128 * (k // 3):128 * (k // 3) + 128], wdn[q][:, k // 3, bass.ds(rE[j] * D, D)],
                start=(k == 0), stop=(k == 5)), htd[j], free)
        dwn[j] = tok
        eng = act
        cp = lambda e: e.activation(yb[:, j % NYB], bank[:, 0:D], ACT.Copy)
        a = yk.free[i] = eng.do(cp, tok, s_yo[j % NYB].last())
        ydone[j] = sp.dma(s_yo[j % NYB], ys[128 * j:128 * j + 128, :], yb[:, j % NYB], a)

    NB = min(NBLK, 2 * NT + 8)
    for j in range(min(NX, NB)):
        xload(j)
    trx(0)
    trx(1)
    for j in range(NB + 2):
        if j < NB:
            gate_up(j)
        if j == 4:
            results()
        if 1 <= j < NB + 1:
            trh_(j - 1)
        if j + 2 < NB:
            trx(j + 2)
        if j >= 2:
            down(j - 2)
        if j + NX < NB:
            xload(j + NX)

    yall = [s.last() for s in s_yo]
    quiet = [dve.last(), act.last(), pe.last()]
    CBF = 3
    Xc = X[:, 0:CBF]
    Yg = sb("Yg", [128, CBF, 4, 2, D]) if False else None
    Y = sb("Y", [128, CBF, 8, D])
    s_cl = [c.stream(f"{tag}cl{i}") for i in range(CBF)]
    s_cg = [c.stream(f"{tag}cg{i}") for i in range(CBF)]
    s_co = [c.stream(f"{tag}co{i}") for i in range(CBF)]
    last = {}
    for g in range(NG):
        z = g % CBF
        ld = sp.dma(s_cl[z], Xc[:, z], xv[g], *quiet, *yall, s_co[z].last())
        for t in range(4):
            for k in range(2):
                pool.do(lambda e, t=t, k=k, g=g, z=z: e.indirect_dma_start(
                    Y[:, z, 2 * t + k, :], None, ys[0:128 * NB, :],
                    bass.IndirectOffsetOnAxis(ap=yi[:, 4 * g + t, k:k + 1], axis=0)), *yall, after["rows"], last.get(g - CBF), mark=False)
                wts, f, _ = pool.items[-1]
                pool.items[-1] = (wts, f, (s_cg[z].sem, 16))
                got = s_cg[z].count()
        for t in range(4):
            a = dv(lambda e, t=t, z=z, g=g: e.scalar_tensor_tensor(
                Xc[:, z, t], Y[:, z, 2 * t], G[:, 4 * g + t, 0:1], Xc[:, z, t], ALU.mult, ALU.add), ld, got, after["gates"])
        for t in range(4):
            a2 = dv(lambda e, t=t, z=z, g=g: e.scalar_tensor_tensor(
                Xc[:, z, t], Y[:, z, 2 * t + 1], G[:, 4 * g + t, 1:2], Xc[:, z, t], ALU.mult, ALU.add), a)
        last[g] = a2
        sp.dma(s_co[z], ov[g], Xc[:, z], a2)
    ctx.close()
    return [s.last() for s in s_co]


def attention(c, B, x1, x2, parts, mdram, cst, w):
    nc, pe, dve, act, pool, sp = c.nc, c.pe, c.dve, c.act, c.pool, c.sp
    ctx = ExitStack()

    def sb(name, shape, dt=F32):
        return ctx.enter_context(nc.sbuf_tensor("at_" + name, shape, dt))

    qst = sb("qst", [99, NS, 2, S], BF16)
    kst = sb("kst", [99, NS, 2, S], BF16)
    P = sb("P", [128, NP, 512])
    NSD = 40
    Sd = sb("Sd", [128, NSD, 128])
    V = sb("V", [128, 2, 8, H, 17])
    XR = sb("XR", [128, 8, D])
    xT = sb("xT", [128, 2, S])
    lat = sb("lat", [DL, S])
    pt = sb("pt", [128, 2, 3, 512], BF16)
    qf = sb("qf", [128, 2, 512])
    OT = sb("OT", [128, 8, D])
    OF = sb("OF", [128, 2, 512])
    Ou = sb("Ou", [128, 2, 512])
    res = sb("res", [128, NR, D])
    ident = sb("ident", [128, 128])
    decn = sb("decn", [128, 512])
    decp = sb("decp", [128, 512])
    Dm = sb("Dm", [128, 128])
    wq = sb("wq", [128, 2, D])
    wk = sb("wk", [128, 2, D])
    wo = sb("wo", [128, 2, D])
    wd = sb("wd", [128, 2, DL])
    wuk = sb("wuk", [DL, D])
    wuv = sb("wuv", [DL, D])
    wkT = Ou[:, 0].rearrange("p (k d) -> p k d", k=2)
    wkv = sb("wkv", [128, 2, DL])
    st = sb("st", [128, 6])
    mv = sb("mv", [128, 8, 2])
    ve = sb("ve", [128, 8])
    sq = sb("sq", [128, 8])
    rs = sb("rs", [128, 8])
    mx = sb("mx", [128, 4, 8, 3])
    m = sb("m", [128, 4, 8])
    mT = sb("mT", [8, 2, 128])
    mp = sb("mp", [8, 2, 3, 128], BF16)
    rc = sb("rc", [128, 4, 4])

    s_w, s_x = (c.stream("at_" + n) for n in ("w", "x"))
    s_m = [c.stream(f"at_m{i}") for i in range(2)]
    s_pt = [c.stream(f"at_pt{i}") for i in range(2)]
    s_st = [c.stream(f"at_st{i}") for i in range(NS)]
    s_mr = [c.stream(f"at_mr{i}") for i in range(NS)]
    s_res = [c.stream(f"at_res{i}") for i in range(NR)]
    s_yr = [c.stream(f"at_yr{i}") for i in range(NR)]

    def fold(a):
        return a.rearrange("(k p) n -> p k n", p=128)

    for dst, src in ((ident[:], cst["ident"]), (decn[:], cst["decn"]), (decp[:], cst["decp"]),
                     (Dm[:], cst["dm"]), (wq[:], fold(w["q"])), (wk[:], fold(w["k"])),
                     (wkT, fold(w["v"])), (wd[:], fold(w["down"])), (wuk[:], w["upk"]),
                     (wuv[:], w["upv"]), (wo[:], fold(w["o"]))):
        loaded = sp.dma(s_w, dst, src)
    ones_k = dve.do(lambda e: e.memset(kst[96:99, :, :, :], 1.0))
    ones_v = dve.do(lambda e: e.memset(V[:, :, :, :, 16:17], 1.0))
    v0 = dve.do(lambda e: e.memset(c.V, 0.0))
    wsum = dve.do(lambda e: e.tensor_tensor(wk[:], wk[:], wkT, ALU.add), loaded)
    wqs = dve.do(lambda e: e.tensor_scalar_mul(wq[:], wq[:], 1.0 / 16.0), loaded)
    fT = {}
    for i in range(2):
        def fill(bank, free, i=i):
            for j in range(2):
                t = c.tr(bank[:, 128 * j:128 * j + 128], wk[:, i, 128 * j:128 * j + 128], ident[:],
                         wsum, loaded, free)
            return t

        def use(bank, tok, i=i):
            fT[i] = dve.do(lambda e: e.tensor_copy(
                Ou[:, 0].rearrange("p (j i q) -> p j i q", j=2, i=2)[:, :, i, :],
                bank[:, 0:256].rearrange("p (j q) -> p j q", j=2)), tok, wsum)
            return fT[i]
        c.unit(fill, use)

    def fill_wkv(bank, free):
        for i in range(2):
            for j in range(2):
                t = c.mm(bank[:, i * DL:(i + 1) * DL], Ou[:, 0, 256 * j + 128 * i:256 * j + 128 * i + 128],
                         wd[:, j, :], fT[0], fT[1], free, start=(j == 0), stop=(j == 1))
        return t

    def use_wkv(bank, tok):
        return dve.do(lambda e: e.tensor_copy(wkv[:], bank[:, 0:128].rearrange("p (k n) -> p k n", k=2)), tok)
    c.unit(fill_wkv, use_wkv)
    setup = dve.last()

    xdone = {}
    vdone = {}
    pdone = {}
    vread = {}

    xl = {}

    def xload(b, *after):
        xl[b] = sp.dma(s_x, XR[:], x1[b].rearrange("(t p) d -> p t d", p=128), *after)
        return xl[b]

    def prep(b):
        ld = xload(b) if b == 0 else xl[b]
        for t in range(8):
            s1 = dve.do(lambda e, t=t: e.bn_stats(st[:], XR[:, t, :]), ld, dve.last())
            ag = dve.do(lambda e, t=t: e.bn_aggr(mv[:, t, :], st[:]), s1)
            if t % 3 == 2:
                yield
        a = dve.do(lambda e: e.tensor_scalar_add(ve[:], mv[:, :, 1], EPS), ag)
        a2 = act.do(lambda e: e.activation(sq[:], ve[:], ACT.Sqrt), a)
        a3 = dve.do(lambda e: e.reciprocal(rs[:], sq[:]), a2)
        n1 = dve.do(lambda e: e.tensor_tensor(sq[:], rs[:], rs[:], ALU.mult), a3)
        n2 = dve.do(lambda e: e.tensor_tensor(sq[:], sq[:], ve[:], ALU.mult), n1)
        n3 = dve.do(lambda e: e.tensor_scalar(sq[:], sq[:], -0.5, 1.5, ALU.mult, ALU.add), n2)
        n4 = dve.do(lambda e: e.tensor_tensor(rs[:], rs[:], sq[:], ALU.mult), n3)
        for t in range(8):
            xn = dve.do(lambda e, t=t: e.tensor_scalar(XR[:, t, :], XR[:, t, :], mv[:, t, 0:1], rs[:, t:t + 1],
                                                       ALU.subtract, ALU.mult), n4, ag)
            if t % 4 == 3:
                yield
        xTd = {}
        for ch in range(2):
            for k in range(2):
                def fill(bank, free, ch=ch, k=k):
                    for t in range(4):
                        tok = c.tr(bank[:, 128 * t:128 * t + 128], XR[:, 4 * ch + t, 128 * k:128 * k + 128],
                                   ident[:], xn, free)
                    return tok

                def use(bank, tok, ch=ch, k=k):
                    xTd[ch] = act.do(lambda e: e.activation(xT[:, k, 512 * ch:512 * ch + 512], bank[:], ACT.Copy),
                                     tok, prepd.get(b - 1))
                    return xTd[ch]
                c.unit(fill, use)
                yield
        xread = pe.last()
        latd = {}
        for ch in range(2):
            def fill(bank, free, ch=ch):
                for k in range(2):
                    tok = c.mm(bank[0:DL, :], wkv[:, k, :], xT[:, k, 512 * ch:512 * ch + 512], xTd[ch], setup, free,
                               start=(k == 0), stop=(k == 1))
                return tok

            def use(bank, tok, ch=ch):
                latd[ch] = act.do(lambda e: e.activation(lat[:, 512 * ch:512 * ch + 512], bank[0:DL, :], ACT.Copy), tok)
                return latd[ch]
            c.unit(fill, use)
            yield
        for kind in range(2):
            for hf in range(2):
                for ch in range(2):
                    def fill(bank, free):
                        sl = slice(512 * ch, 512 * ch + 512)
                        if kind == 0:
                            for k in range(2):
                                tok = c.mm(bank[:], wq[:, k, 128 * hf:128 * hf + 128], xT[:, k, sl], xTd[ch], wqs, free,
                                           start=(k == 0), stop=(k == 1))
                        else:
                            tok = c.mm(bank[:], wuk[:, 128 * hf:128 * hf + 128], lat[:, sl], latd[ch], free)
                        return tok

                    def use(bank, tok):
                        prev = st_pool.get("q")
                        for v in range(2):
                            st_pool["f"] = act.do(lambda e, v=v, far=far: e.activation(
                                qf[:, v], bank[:], ACT.Copy, scale=far[v]), tok, prev)
                        return st_pool["f"]
                    far = (FAR[ch], FAR[1 - ch])
                    c.unit(fill, use)
                    yield
                    ready = st_pool["f"]
                    a = [pool.do(lambda e, v=v: e.tensor_tensor(qf[:, v], qf[:, v], (decn, decp)[v][:], ALU.mult),
                                 ready, loaded) for v in range(2)]
                    yield
                    yield
                    for p in range(2):
                        a = [act.do(lambda e, v=v, p=p: e.activation(pt[:, v, p, :], qf[:, v], ACT.Copy),
                                    a[v], st_pool.get(("d", v))) for v in range(2)]
                        a = [pool.do(lambda e, v=v, p=p: e.tensor_tensor(
                            qf[:, v] if p == 0 else pt[:, v, 2, :], qf[:, v], pt[:, v, p, :], ALU.subtract), a[v])
                            for v in range(2)]
                        yield
                        if p == 0:
                            yield
                    st_pool["q"] = a[1]
                    for v in range(2):
                        for p in range(3):
                            dst = parts[b % 2, kind, 8 * hf:8 * hf + 8, p, :, v, 512 * ch:512 * ch + 512]
                            st_pool[("d", v)] = sp.dma(s_pt[v], dst, pt[:, v, p, :], a[v], stfree.get(b - 2))
        pdone[b] = [s_pt[0].last(), s_pt[1].last()]
        if b + 1 < B:
            xload(b + 1, xread)
        for t2 in range(4):
            def fill(bank, free):
                for j in range(2):
                    t = 2 * t2 + j
                    tok = c.mm(bank[:, 256 * j:256 * j + 256], lat[:, 128 * t:128 * t + 128], wuv[:], latd[t // 4], free)
                return tok

            def use(bank, tok):
                vdone[b] = act.do(lambda e, t2=t2, b=b: e.activation(
                    V[:, b % 2, 2 * t2:2 * t2 + 2, :, 0:16],
                    bank[:].rearrange("p (t h d) -> p t h d", t=2, h=H), ACT.Copy), tok, vread.get(b - 2))
                return vdone[b]
            c.unit(fill, use)
            yield
        prepd[b] = pe.last()

    prepd = {}
    st_pool = {}
    stfree = {}
    filled = {}
    qpat = ((0, 48), (48, 80), (80, 96))
    NH = B * H

    def fill_stack(n):
        b, h = divmod(n, H)
        s = n % NS
        free = free_of(n)
        more = [*pdone[b], free]
        src = parts[b % 2]
        qd = qst[:, s, :, :]
        kd = kst[:, s, :, :]
        for p, (r0, r1) in enumerate(((0, 3), (3, 5), (5, 6))):
            for r in range(r0, r1):
                sp.dma(s_st[s], qd[16 * r:16 * r + 16], src[0, h, p], *more)
        sp.dma(s_st[s], kd[0:48], src[1, h].rearrange("p d v t -> (p d) v t"), *more)
        sp.dma(s_st[s], kd[48:80], src[1, h, 0:2].rearrange("p d v t -> (p d) v t"), *more)
        filled[n] = sp.dma(s_st[s], kd[80:96], src[1, h, 0], *more)
        if h == H - 1:
            stfree[b] = filled[n]

    tdone = {}
    sdfree = [None] * NSD
    sdlist = list(range(NSD))
    sdslot = {}
    sdtok = {}
    mrow = {}
    mdone = {}

    def pieces(t, c0, c1, diag_last):
        out = []
        if diag_last:
            left = [(0, 0, 128 * t, 0), (128 * t, 128 * t + 128, 896 - 128 * t, 1), (896, 128 * t, 128, 0)]
        else:
            left = [(0, 0, 128 * t, 0), (128 * t + 128, 128 * t + 128, 896 - 128 * t, 1)]
        for col, key, n, side in left:
            a, z = max(col, c0), min(col + n, c1)
            if z > a:
                out.append((a, key + a - col, z - a, side))
        return out

    def s_stream():
        late = []
        for n in range(NH):
            s, z = n % NS, n % 4
            assert n in filled
            for t in range(8):
                slot = sdlist.pop(0)
                sdslot[(n, t)] = slot
                for u in range(2):
                    def fill(bank, free):
                        for col, key, ln, side in pieces(t, 512 * u, 512 * u + 512, True):
                            tok = c.mm(bank[:, col - 512 * u:col - 512 * u + ln],
                                       qst[0:96, s, side, 128 * t:128 * t + 128],
                                       kst[0:96, s, 1 - side, key:key + ln], filled[n], free)
                        return tok

                    def use(bank, tok, s=s, z=z, t=t, slot=slot):
                        if u == 0:
                            return dve.do(lambda e: e.tensor_reduce(
                                mx[:, z, t, 0:1], bank[:, 0:512], op=ALU.max, axis=AX.X), tok, mdone.get(n - 4))
                        dve.do(lambda e: e.tensor_reduce(
                            mx[:, z, t, 1:2], bank[:, 0:384], op=ALU.max, axis=AX.X), tok)
                        sdtok[(n, t)] = dve.do(lambda e: e.tensor_tensor_reduce(
                            out=Sd[:, slot, :], in0=bank[:, 384:512], in1=Dm[:], scale=1.0, scalar=-3.0e38,
                            op0=ALU.mult, op1=ALU.max, accum_out=mx[:, z, t, 2:3]), tok, sdfree[slot], loaded)
                        return sdtok[(n, t)]
                    c.unit(fill, use)
                    sdone[0] += 1
                    yield
                if late and t in (0, 1, 2):
                    late.pop(0)()
            late = maxima(n)
        for f in late:
            f()

    def maxima(n):
        s, z = n % NS, n % 4
        mdone[n] = dve.do(lambda e: e.tensor_reduce(m[:, z, :], mx[:, z], op=ALU.max, axis=AX.X),
                          sdtok[(n, 7)], mread.get(n - 4))
        for t in range(8):
            slot = sdslot[(n, t)]
            sdtok[(n, t)] = pool.do(lambda e, slot=slot, t=t: e.tensor_tensor(
                Sd[:, slot, :], Sd[:, slot, :], m[:, z, t:t + 1].to_broadcast([128, 128]), ALU.subtract), mdone[n])
        mread[n] = sdtok[(n, 7)]
        y = n % 2
        t0 = {}

        def turn():
            def fill(bank, free):
                mt = c.tr(bank[0:8, 0:128], m[:, z, :], ident[:], mdone[n], free)
                mreadpe[n] = mt
                return mt

            def use(bank, tok):
                t0[0] = dve.do(lambda e: e.tensor_scalar_mul(mT[:, y], bank[0:8, 0:128], -1.0), tok)
                return t0[0]
            c.unit(fill, use)

        def split():
            t1 = dve.do(lambda e: e.tensor_copy(mp[:, y, 0, :], mT[:, y]), t0[0], wrote.get(n - 2))
            t2 = dve.do(lambda e: e.tensor_tensor(mT[:, y], mT[:, y], mp[:, y, 0, :], ALU.subtract), t1)
            t3 = dve.do(lambda e: e.tensor_copy(mp[:, y, 1, :], mT[:, y]), t2)
            t0[1] = dve.do(lambda e: e.tensor_tensor(mp[:, y, 2, :], mT[:, y], mp[:, y, 1, :], ALU.subtract), t3)

        def send():
            wrote[n] = sp.dma(s_m[y], mdram[z], mp[:, y], t0[1], mrow.get(n - 4))
            for v in range(2):
                mrow[n] = sp.dma(s_mr[s], qst[96:99, s, v, :].rearrange("c (t q) -> c t q", q=128),
                                 mdram[z].rearrange("t c q -> c t q"), wrote[n], free_of(n))
        return [turn, split, send]

    def free_of(n):
        return tdone[(n - NS) // 4] if n >= NS else None

    mread, mreadpe, wrote = {}, {}, {}
    sdone = [0]
    pfree = [None] * NP
    pvfree = [v0]
    late_work = []

    def t_stream():
        pn = tn = 0
        nt = len(c.T)
        ready, bufs = [], []
        tfree = [None] * nt
        for g in range(NH // 4):
            for qh in range(2):
                for kk in range(8):
                    kb = (kk + 4 * qh) % 8
                    for hh in range(4):
                        n = 4 * g + hh
                        s = n % NS
                        i = tn % nt
                        tn += 1
                        bank = c.T[i]
                        tok = None
                        for col, q0, ln, side in pieces(kb, 512 * qh, 512 * qh + 512, False):
                            col -= 512 * qh
                            tok = c.mm(bank[:, col:col + ln], kst[0:99, s, side, 128 * kb:128 * kb + 128],
                                       qst[0:99, s, 1 - side, q0:q0 + ln], filled[n], mrow[n], ones_k, tfree[i])
                        if kb // 4 == qh:
                            slot = sdslot[(n, kb)]
                            col = 128 * (kb % 4)
                            tok = c.tr(bank[:, col:col + 128], Sd[:, slot, :], ident[:], sdtok[(n, kb)], tfree[i])
                            sdfree[slot] = tok
                            sdlist.append(slot)
                        pi = pn % NP
                        pn += 1
                        ex = act.do(lambda e, pi=pi, bank=bank: e.activation(P[:, pi, :], bank, ACT.Exp), tok, pfree[pi])
                        tfree[i] = ex
                        bufs.append((pi, ex))
                        if kk == 7 and hh == 3 and qh == 1:
                            tdone[g] = tok
                        yield g
                        if ready and hh == 1:
                            weigh(*ready)
                            ready = []
                    ready, bufs = [g, qh, kk, kb, bufs], []
        weigh(*ready)

    def weigh(g, qh, kk, kb, pv):
        b = g // 4
        for hh in range(4):
            pi, ex = pv[hh]
            h = (4 * g + hh) % H
            tok = pfree[pi] = c.mm(c.V[32 * hh:32 * hh + 17, :], V[:, b % 2, kb, h, :], P[:, pi, :],
                                   ex, vdone[b], ones_v, pvfree[0], start=(kk == 0), stop=(kk == 7))
        if kk == 7:
            vread[b] = tok
            pvfree[0] = act.do(lambda e: e.activation(Ou[:, qh], c.V, ACT.Copy), tok, wfold[("o", qh)])
            late_work.append(normed(g, qh, pvfree[0]))

    def normed(g, qh, ev):
        b = g // 4

        def fill(bank, free):
            for t in range(4):
                tok = c.tr(bank[:, 128 * t:128 * t + 128], Ou[:, qh, 128 * t:128 * t + 128], ident[:], ev, free)
            wfold[("o", qh)] = tok
            return tok

        def use(bank, tok):
            v4 = bank.rearrange("p (t h x) -> p t h x", t=4, h=4)
            r1 = dve.do(lambda e: e.reciprocal(rc[:], v4[:, :, :, 16]), tok, wfold.get("rc"))
            g4 = 64 * (g % 4)
            wfold["rc"] = dve.do(lambda e: e.tensor_tensor(
                OT[:, 4 * qh:4 * qh + 4, g4:g4 + 64].rearrange("p t (h x) -> p t h x", h=4),
                v4[:, :, :, 0:16], rc[:].rearrange("p t (h o) -> p t h o", o=1).to_broadcast([128, 4, 4, 16]),
                ALU.mult), r1, wfold.get("otr"))
            return wfold["rc"]
        c.unit(fill, use)
        yield
        if g % 4 < 3 or qh == 0:
            return
        otd = wfold["rc"]
        resl = {}

        def resload(tt):
            r = tt % NR
            resl[tt] = sp.dma(s_res[r], res[:, r, :], x1[b, 128 * tt:128 * tt + 128, :], s_yr[r].last())
        for tt in range(NR):
            resload(tt)
        for ch in range(2):
            for k in range(2):
                def fill(bank, free):
                    for t in range(4):
                        tok = c.tr(bank[:, 128 * t:128 * t + 128], OT[:, 4 * ch + t, 128 * k:128 * k + 128],
                                   ident[:], otd, free)
                    wfold["otr"] = tok
                    return tok

                def use(bank, tok):
                    wfold["of"] = act.do(lambda e, k=k: e.activation(OF[:, k, :], bank[:], ACT.Copy), tok, wfold.get("pj"))
                    return wfold["of"]
                c.unit(fill, use)
                yield
            for t in range(4):
                tt = 4 * ch + t
                r = tt % NR
                ld = resl.pop(tt)

                def fill(bank, free):
                    for k in range(2):
                        tok = c.mm(bank[:, 0:D], OF[:, k, 128 * t:128 * t + 128], wo[:, k, :], wfold["of"], free,
                                   start=(k == 0), stop=(k == 1))
                    wfold["pj"] = tok
                    return tok

                def use(bank, tok):
                    rr = dve.do(lambda e, r=r: e.tensor_tensor(res[:, r, :], bank[:, 0:D], res[:, r, :], ALU.add), tok, ld)
                    sp.dma(s_yr[r], x2[b, 128 * tt:128 * tt + 128, :], res[:, r, :], rr)
                    return rr
                c.unit(fill, use)
                yield
                if 0 < tt and tt - 1 + NR < 8:
                    resload(tt - 1 + NR)

    wfold = {("o", 0): setup, ("o", 1): setup}

    for _ in prep(0):
        pass
    nf = 0
    while nf < min(NS, NH):
        if nf // H not in pdone:
            break
        fill_stack(nf)
        nf += 1
    ss = s_stream()
    LEAD = 8
    while sdone[0] < min(2 * (32 + LEAD), 16 * NH):
        next(ss)
    gp, gb = None, 1
    step = 0
    for g in t_stream():
        if step % 64 in (4, 16, 28, 44) and g and nf < NH:
            while nf // H not in pdone:
                next(gp)
            fill_stack(nf)
            nf += 1
        if gp is None and gb < B and g >= 4 * gb - 5 and step % 64 >= 16:
            gp = prep(gb)
        next(ss, None)
        if step % 2 == 0:
            if gp is not None and next(gp, 1) == 1:
                gp, gb = None, gb + 1
        elif late_work and (gp is None or step % 4 == 1) and next(late_work[0], 1) == 1:
            late_work.pop(0)
        step += 1
    for _ in ss:
        pass
    for w_ in late_work:
        for _ in w_:
            pass
    ctx.close()
    return [s.last() for s in s_yr]


def consts():
    t = np.arange(S, dtype=np.float64) - (S / 4 - 0.5)
    i = np.arange(128, dtype=np.float64)
    e = np.arange(E, dtype=np.float32)
    misc = np.concatenate([np.tile(e, (128, 1)), np.tile(e * CAP, (128, 1)), i[:, None]], 1).astype(np.float32)
    return {
        "tri": (i[:, None] < i[None, :]).astype(np.float32),
        "misc": misc,
        "jf": np.arange(NBLK, dtype=np.float32)[None, :],
        "ident": np.eye(128, dtype=np.float32),
        "decn": np.tile(np.exp(-LAM * t[:512]).astype(np.float32), (128, 1)),
        "decp": np.tile(np.exp(LAM * t[:512]).astype(np.float32), (128, 1)),
        "dm": np.exp(np.minimum(0.0, 2 * LAM * (i[:, None] - i[None, :]))).astype(np.float32),
    }


_INS = ['L0_attn_x', 'L0_attn_W_q', 'L0_attn_W_k', 'L0_attn_W_v', 'L0_attn_W_o', 'L0_attn_W_down_kv', 'L0_attn_W_up_k',
        'L0_attn_W_up_v', 'L0_ffn_router_w', 'L0_ffn_router_b', 'L0_ffn_we_gate', 'L0_ffn_we_up', 'L0_ffn_we_down']
_ROUTE = ("ident", "tri", "misc", "jf")


def program(nc, a, cst, out):
    B = 16
    x, wq, wk, wv, wo, wdn, wuk, wuv, rw, rb, eg, eu, ed = a
    with ExitStack() as ctx:
        c = Core(nc, ctx)
        x1 = nc.dram_tensor("x1", [B, S, D], F32).ap()
        x2 = nc.dram_tensor("x2", [B, S, D], F32).ap()
        xs = nc.dram_tensor("xs", [E * CAP, D], F32).ap()
        ys = nc.dram_tensor("ys", [NBLK * 128, D], F32).ap()
        parts = nc.dram_tensor("parts", [2, 2, H, 3, HD, 2, S], BF16).ap()
        mdram = nc.dram_tensor("mdram", [4, 8, 3, 128], BF16).ap()
        we = {"rw": rw, "rb": rb, "g": eg, "u": eu, "d": ed}
        wa = {"q": wq, "k": wk, "v": wv, "o": wo, "down": wdn, "upk": wuk, "upv": wuv}

        def flat(t):
            return t.rearrange("b s d -> (b s) d")
        moe(c, B * S // 128, flat(x), flat(x1), xs, ys, cst, we, [], "m1")
        c.meet()
        attention(c, B, x1, x2, parts, mdram, cst, wa)
        c.meet()
        moe(c, B * S // 128, flat(x2), flat(out), xs, ys, cst, we, [], "m2")
        ends = [s.last() for s in c.streams if s.n]
        block = ctx.enter_context(nc.Block())

        @block.sync
        def _(e):
            c.sp.run(e)
            for sem, n, _k in ends:
                e.wait_ge(sem, n)

        @block.scalar
        def _(e):
            c.act.run(e)

        @block.vector
        def _(e):
            c.dve.run(e)

        @block.tensor
        def _(e):
            c.pe.run(e)

        @block.gpsimd
        def _(e):
            c.pool.run(e)


def kernel(**inputs):
    import concourse.bacc as _bacc
    from concourse.bass_utils import run_bass_kernel_spmd as _run

    nc = _bacc.Bacc("TRN2", target_bir_lowering=False, num_devices=1)
    arrays, args = {}, []
    for name in _INS:
        v = np.ascontiguousarray(inputs[name])
        arrays[f"in_{name}"] = v
        args.append(nc.dram_tensor(f"in_{name}", v.shape, mybir.dt.from_np(v.dtype), kind="ExternalInput").ap())
    cst = {}
    for name, v in consts().items():
        arrays[f"const_{name}"] = v
        cst[name] = nc.dram_tensor(f"const_{name}", v.shape, F32, kind="ExternalInput").ap()
    out = nc.dram_tensor("out", (16, S, D), F32, kind="ExternalOutput").ap()
    program(nc, args, cst, out.rearrange("b s d -> b s d"))
    r = _run(nc, [arrays], core_ids=[0])
    return r.results[0]["out"]
```

```python
import concourse.bass as bass
from concourse import mybir
from contextlib import ExitStack
import numpy as np

F32 = mybir.dt.float32
BF16 = mybir.dt.bfloat16
F32R = mybir.dt.float32r
I32 = mybir.dt.int32
U32 = mybir.dt.uint32
ACT = mybir.ActivationFunctionType
ALU = mybir.AluOpType
AX = mybir.AxisListType

D = 256
S = 1024
H = 16
HD = 16
DL = 64
E = 8
LAM = 0.01
EPS = 1e-5
NS = 10
FAR = (float(np.exp(LAM * S / 4)), float(np.exp(-LAM * S / 4)))
NP = 12
NR = 3


class Queue:

    def __init__(self, sem):
        self.sem, self.n, self.items, self.seen, self.hold = sem, 0, [], {}, []

    def do(self, f, *after, mark=True):
        waits = []
        after, self.hold = [*self.hold, *after], []
        for tok in after:
            if tok is None:
                continue
            s, v, key = tok
            if self.seen.get(key, 0) < v:
                self.seen[key] = v
                waits.append((s, v))
        tok = None
        if mark:
            self.n += 1
            tok = (self.sem, self.n, id(self.sem))
        self.items.append((waits, f, (self.sem, 1) if mark else None))
        return tok

    def dma(self, stream, out, in_, *after):
        self.do(lambda e: e.dma_start(out, in_), *after, mark=False)
        waits, f, _ = self.items[-1]
        self.items[-1] = (waits, f, (stream.sem, 16))
        return stream.count()

    def last(self):
        return (self.sem, self.n, id(self.sem)) if self.n else None

    def run(self, eng):
        for waits, f, inc in self.items:
            for s, v in waits:
                eng.wait_ge(s, v)
            ins = f(eng)
            if inc:
                ins.then_inc(*inc)


class Stream:

    def __init__(self, sem):
        self.sem, self.n = sem, 0

    def count(self):
        self.n += 16
        return self.last()

    def last(self):
        return (self.sem, self.n, id(self.sem)) if self.n else None


class Core:

    def __init__(self, nc, ctx):
        self.nc, self.ctx, self.streams = nc, ctx, []
        self.pe, self.dve, self.act, self.pool, self.sp = (
            Queue(self.sem(n)) for n in ("s_pe", "s_dve", "s_act", "s_pool", "s_sp"))
        ps = ctx.enter_context(nc.psum_tensor("psum", [128, 4096], F32))
        self.bank = [ps[:, 512 * i:512 * i + 512] for i in range(8)]
        self.A = self.bank[0:4]
        self.T = self.bank[4:7]
        self.V = self.bank[7]
        self.a_n = 0
        self.a_free = [None] * len(self.A)

    def sem(self, name):
        return self.ctx.enter_context(self.nc.semaphore(name))

    def stream(self, name):
        self.streams.append(Stream(self.sem(name)))
        return self.streams[-1]

    def unit(self, fill, use):
        self.empty(*self.filled(fill), use)

    def filled(self, fill):
        i = self.a_n % len(self.A)
        self.a_n += 1
        return i, fill(self.A[i], self.a_free[i])

    def empty(self, i, tok, use):
        self.a_free[i] = use(self.A[i], tok)

    def meet(self):
        at = [q.last() for q in (self.pe, self.dve, self.act, self.pool, self.sp)]
        at += [s.last() for s in self.streams]
        for q in (self.pe, self.dve, self.act, self.pool, self.sp):
            q.hold = at

    def mm(self, out, lhsT, rhs, *after, start=True, stop=True, mark=True):
        return self.pe.do(lambda e: e.matmul(out, lhsT, rhs, start=start, stop=stop), *after, mark=mark)

    def tr(self, out, in_, ident, *after, mark=True):
        return self.pe.do(lambda e: e.transpose(out, in_, ident), *after, mark=mark)


NBLK = 272
XROWS = 16 * 128 * 89
HALVES = ((0, 0), (0, 1), (1, 0)) * 2


class Ring:

    def __init__(self, banks):
        self.banks, self.n, self.free = banks, 0, [None] * len(banks)

    def take(self):
        i = self.n % len(self.banks)
        self.n += 1
        return i, self.banks[i], self.free[i]


def moe(c, NT, xin, out, xs, ys, cst, w, begin, tag, tables=None, cuts=()):
    nc, pe, dve, act, pool, sp = c.nc, c.pe, c.dve, c.act, c.pool, c.sp
    ctx = ExitStack()
    cuts = (0, *cuts, NT // 4)
    H = len(cuts) - 1
    CB = 4 * max(b - a for a, b in zip(cuts, cuts[1:])) + 1
    CAP = 128 * CB
    NR_ = H * E

    def sb(name, shape, dt=F32):
        return ctx.enter_context(nc.sbuf_tensor(tag + name, shape, dt))

    wgu = [sb(f"wgu{i}", [128, 2, E * 512], F32R) for i in range(2)]
    wdn = [sb(f"wdn{i}", [128, 2, E * D], F32R) for i in range(2)]
    wst = sb("wst", [128, 2, 2, D])
    rw = sb("rw", [128, 2, E])
    rb = sb("rb", [128, E])
    ident = sb("ident", [128, 128])
    tri = sb("tri", [128, 128], BF16)
    ones = sb("ones", [128, 128], BF16)
    trif = sb("trif", [128, 128])
    misc = sb("misc", [128, 17])
    iota8, region, iotap = misc[:, 0:8], misc[:, 0:NR_], misc[:, 16:17]
    first = sb("first", [128, NR_])
    fin = sb("fin", [128, NR_])
    jf = sb("jf", [1, NBLK])
    zero = sb("zero", [128, D])
    P = sb("P", [128, NT, 2])
    EX = sb("EX", [128, NT, 2])
    M = sb("M", [128, NT, 2])
    XB, Z = 8, 4
    X = sb("X", [128, XB, 4, D])
    xT = sb("xT", [128, Z, 2, 512])
    st = sb("st", [128, Z, 4, 6])
    mv = sb("mv", [128, Z, 4, 2])
    ve = sb("ve", [128, Z, 4])
    sq = sb("sq", [128, Z, 4])
    rs = sb("rs", [128, Z, 4])
    lg = sb("lg", [128, Z, 4, E])
    m8 = sb("m8", [128, Z, 4, 8])
    i8 = sb("i8", [128, Z, 4, 8], U32)
    OH = sb("OH", [128, Z, 4, 2, E])
    O = sb("O", [128, Z, 4, E], BF16)
    base = sb("base", [128, 2, E])
    rk = sb("rk", [128, Z, 4, E])
    pr = sb("pr", [128, Z, 4, 2, E])
    idx = sb("idx", [128, XB, 4, 2], U32)
    s_w, s_pad = (c.stream(tag + n) for n in ("w", "pad"))
    s_ld = [c.stream(f"{tag}ld{i}") for i in range(XB)]
    s_sc = [c.stream(f"{tag}sc{i}") for i in range(XB)]

    def dv(f, *after):
        return dve.do(f, *after)

    ldc = None
    for dst, src in ((ident[:], cst["ident"]), (trif[:], cst["tri"]), (misc[:], cst["misc"]), (jf[:], cst["jf"]),
                     (rw[:], w["rw"].rearrange("(k p) n -> p k n", p=128)),
                     (rb[:], w["rb"].rearrange("(o n) -> o n", o=1).to_broadcast([128, E]))):
        ldc = sp.dma(s_w, dst, src, *begin)
    k1 = dv(lambda e: e.tensor_copy(tri[:], trif[:]), ldc)
    k2 = dv(lambda e: e.memset(ones[:], 1.0))
    k3 = dv(lambda e: e.memset(zero[:], 0.0))
    fs = dv(lambda e: e.tensor_scalar_mul(first[:], region, float(CAP)), ldc)
    bt = dv(lambda e: e.tensor_copy(base[:, 0, :], first[:, 0:E]), fs)

    xv = xin.rearrange("(g t p) d -> g p t d", p=128, t=4)
    ov = None if tables else out.rearrange("(g t p) d -> g p t d", p=128, t=4)
    NG = NT // 4
    ring = Ring(c.bank)
    okd = {}
    scat = {}
    loads = {}

    def load(g):
        loads[g] = sp.dma(s_ld[g % XB], X[:, g % XB], xv[g], scat.get(g - XB))
    for g in range(min(XB, NG)):
        load(g)
    tb = {}
    bts = [bt]

    def route(g):
        z, xb = g % Z, g % XB
        zb = g % 2
        pz = tb.get(g - Z)
        for t in range(4):
            a = dv(lambda e, t=t, z=z, xb=xb: e.bn_stats(st[:, z, t, :], X[:, xb, t, :]), loads[g], pz)
        for t in range(4):
            a2 = dv(lambda e, t=t, z=z: e.bn_aggr(mv[:, z, t, :], st[:, z, t, :]), a)
        a = dv(lambda e, z=z: e.tensor_scalar_add(ve[:, z, :], mv[:, z, :, 1], EPS), a2)
        yield
        q = act.do(lambda e, z=z: e.activation(sq[:, z, :], ve[:, z, :], ACT.Sqrt), a, pz)
        yield
        a = dv(lambda e, z=z: e.reciprocal(rs[:, z, :], sq[:, z, :]), q)
        a = dv(lambda e, z=z: e.tensor_tensor(sq[:, z, :], rs[:, z, :], rs[:, z, :], ALU.mult), a)
        a = dv(lambda e, z=z: e.tensor_tensor(sq[:, z, :], sq[:, z, :], ve[:, z, :], ALU.mult), a)
        a = dv(lambda e, z=z: e.tensor_scalar(sq[:, z, :], sq[:, z, :], -0.5, 1.5, ALU.mult, ALU.add), a)
        a = dv(lambda e, z=z: e.tensor_tensor(rs[:, z, :], rs[:, z, :], sq[:, z, :], ALU.mult), a)
        for t in range(4):
            xn = dv(lambda e, t=t, z=z, xb=xb: e.tensor_scalar(X[:, xb, t, :], X[:, xb, t, :], mv[:, z, t, 0:1],
                                                             rs[:, z, t:t + 1], ALU.subtract, ALU.mult), a)
        yield
        for k in range(2):
            i, bank, free = ring.take()
            for t in range(4):
                tok = c.tr(bank[:, 128 * t:128 * t + 128], X[:, xb, t, 128 * k:128 * k + 128], ident[:], xn, free, ldc)
            ring.free[i] = act.do(lambda e, k=k, z=z, bank=bank: e.activation(xT[:, z, k, :], bank, ACT.Copy),
                                  tok, okd.get(g - Z))
        xtd = ring.free[i]
        yield
        i, bank, free = ring.take()
        for t in range(4):
            for k in range(2):
                tok = c.mm(bank[:, E * t:E * t + E], xT[:, z, k, 128 * t:128 * t + 128], rw[:, k, :], xtd, free,
                           start=(k == 0), stop=(k == 1))
        okd[g] = tok
        yield
        a = ring.free[i] = dv(lambda e, z=z, bank=bank: e.tensor_tensor(
            lg[:, z], bank[:, 0:32].rearrange("p (t e) -> p t e", t=4),
            rb[:].rearrange("p (o e) -> p o e", o=1).to_broadcast([128, 4, E]), ALU.add), tok)
        for t in range(4):
            b1 = dv(lambda e, t=t, z=z: e.max(m8[:, z, t, :], lg[:, z, t, :]), a)
        for t in range(4):
            b2 = dv(lambda e, t=t, z=z: e.max_index(i8[:, z, t, :], m8[:, z, t, :], lg[:, z, t, :]), b1)
        dv(lambda e, z=z, g=g: e.tensor_copy(M[:, 4 * g:4 * g + 4, :], m8[:, z, :, 0:2]), b1)
        b3 = dv(lambda e, z=z, g=g: e.tensor_copy(EX[:, 4 * g:4 * g + 4, :], i8[:, z, :, 0:2]), b2)
        b4 = dv(lambda e, z=z, g=g: e.tensor_tensor(
            OH[:, z], EX[:, 4 * g:4 * g + 4, :].rearrange("p t (k o) -> p t k o", o=1).to_broadcast([128, 4, 2, E]),
            iota8.rearrange("p (a b e) -> p a b e", a=1, b=1).to_broadcast([128, 4, 2, E]), ALU.is_equal), b3)
        b5 = dv(lambda e, z=z: e.tensor_tensor(O[:, z], OH[:, z, :, 0, :], OH[:, z, :, 1, :], ALU.add), b4, tb.get(("pe", g - Z)))
        yield
        i, bank, free = ring.take()
        r4 = bank[:, 0:32].rearrange("p (t e) -> p t e", t=4)
        c.mm(r4, tri[:], O[:, z], b5, free, k1, k2, start=True, stop=False)
        for t in range(3):
            c.mm(r4[:, t + 1:4, :], ones[:], O[:, z, t:t + 1, :].to_broadcast([128, 3 - t, E]), start=False, stop=(t == 2))
        for t in range(4):
            tok = c.mm(bank[:, 32:40], ones[:], O[:, z, t, :], start=(t == 0), stop=(t == 3))
        tb[("pe", g)] = tok
        yield
        b6 = dv(lambda e, z=z, zb=zb, r4=r4: e.tensor_tensor(
            rk[:, z], r4, base[:, zb].rearrange("p (o e) -> p o e", o=1).to_broadcast([128, 4, E]), ALU.add), tok, bts[0])
        bts[0] = ring.free[i] = dv(lambda e, zb=zb, bank=bank: e.tensor_tensor(base[:, 1 - zb], base[:, zb], bank[:, 32:40], ALU.add),
                               b6)
        if g + 1 in cuts:
            part = cuts.index(g + 1)
            bts[0] = dv(lambda e: e.tensor_copy(fin[:, E * part - E:E * part], base[:, 1 - zb]), bts[0])
            if part < H:
                bts[0] = dv(lambda e: e.tensor_copy(base[:, 1 - zb], first[:, E * part:E * part + E]), bts[0])
        b7 = dv(lambda e, z=z: e.tensor_tensor(
            pr[:, z], OH[:, z], rk[:, z].rearrange("p t (o e) -> p t o e", o=1).to_broadcast([128, 4, 2, E]), ALU.mult), b6)
        b8 = dv(lambda e, z=z, g=g: e.tensor_reduce(P[:, 4 * g:4 * g + 4, :], pr[:, z], op=ALU.add, axis=AX.X), b7)
        b9 = dv(lambda e, g=g, xb=xb: e.tensor_copy(idx[:, xb], P[:, 4 * g:4 * g + 4, :]), b8, scat.get(g - XB))
        tb[g] = b9
        for t in range(4):
            for k in range(2):
                pool.do(lambda e, t=t, k=k, xb=xb: e.indirect_dma_start(
                    xs, bass.IndirectOffsetOnAxis(ap=idx[:, xb, t, k:k + 1], axis=0), X[:, xb, t, :], None),
                    b9, k3, *(begin if g == 0 else ()), mark=False)
                wts, f, _ = pool.items[-1]
                pool.items[-1] = (wts, f, (s_sc[xb].sem, 16))
                scat[g] = s_sc[xb].count()

    s_ws = [c.stream(f"{tag}ws{i}") for i in range(2)]
    wfree = [None, None]
    wl = None

    def high(i, ld, dst):
        return act.do(lambda e: e.activation(dst[0], wst[:, i], ACT.Copy), ld)

    def low(i, hi, dst):
        lo = dv(lambda e: e.tensor_tensor(dst[1], wst[:, i], dst[0].bitcast(F32), ALU.subtract), hi)
        wfree[i] = lo
        return lo

    shares, wlow = [], []
    for x in range(E):
        for h in range(2):
            shares.append((w["gu"[h]][x], [t[:].rearrange("p k (e h n) -> p k e h n", e=E, h=2)[:, :, x, h, :] for t in wgu]))
        shares.append((w["d"][x], [t[:].rearrange("p k (e n) -> p k e n", e=E)[:, :, x, :] for t in wdn]))

    def weights():
        def fetch(i):
            return sp.dma(s_ws[i % 2], wst[:, i % 2], shares[i][0].rearrange("(k p) n -> p k n", p=128), wfree[i % 2], *begin)
        nxt = fetch(0)
        for i, (_s, dst) in enumerate(shares):
            ld, nxt = nxt, None
            if wlow:
                wlow.pop()()
            if i + 1 < len(shares):
                nxt = fetch(i + 1)
            hi = high(i % 2, ld, dst)
            wlow.append(lambda i=i, hi=hi, dst=dst: low(i % 2, hi, dst))
            yield
        wlow.pop()()
    wgen = weights()
    live = {}
    for g in range(NG + 4):
        while len(loads) < NG and len(loads) - XB in scat:
            load(len(loads))
        if g < NG:
            live[g] = route(g)
        for back, steps in ((4, 1), (2, 2), (3, 2), (1, 1), (0, 2)):
            if 0 <= g - back < NG:
                for _s in range(steps):
                    next(live[g - back], None)
        if g >= 5:
            next(wgen, None)
    for _s in wgen:
        pass
    wl = dve.last()
    bt = bts[0]
    cnt = sb("cnt", [128, NR_])
    nbi = sb("nbi", [128, NR_], I32)
    nb = sb("nb", [128, NR_])
    bend = sb("bend", [128, NR_])
    ysh = sb("ysh", [128, NR_])
    dl = sb("dl", [128, NR_])
    tot = sb("tot", [128, 1])
    padf = sb("padf", [128, NR_])
    padi = sb("padi", [128, NR_], U32)
    jt = sb("jt", [1, 4, NBLK])
    tabE = sb("tabE", [1, NBLK], I32)
    tabI = sb("tabI", [1, NBLK], I32)
    tabR = sb("tabR", [1, NBLK], I32)
    G = sb("G", [128, NT, 2])
    T1 = sb("T1", [128, NT, 2])
    yi = sb("yi", [128, NT, 2], U32)
    a = dv(lambda e: e.tensor_scalar(padf[:], fin[:], iotap, None, ALU.add), bt)
    padr = dv(lambda e: e.tensor_copy(padi[:], padf[:]), a)
    for x in range(NR_):
        def pad(e, x=x):
            r = e.value_load(padi[0:1, x:x + 1], min_val=0, max_val=NR_ * CAP - 128)
            return e.dma_start(xs[bass.ds(r, 128), :], zero[:])
        sp.do(pad, padr, k3, mark=False)
        wts, f, _ = sp.items[-1]
        sp.items[-1] = (wts, f, (s_pad.sem, 16))
        pads = s_pad.count()
    scattered = [s.last() for s in s_sc] + [pads]
    a = dv(lambda e: e.tensor_tensor(cnt[:], fin[:], first[:], ALU.subtract), bt)
    a = dv(lambda e: e.tensor_scalar_add(cnt[:], cnt[:], 127.0), a)
    a = dv(lambda e: e.tensor_copy(nbi[:], cnt[:]), a)
    a = dv(lambda e: e.tensor_single_scalar(nbi[:], nbi[:], 7, ALU.arith_shift_right), a)
    a = dv(lambda e: e.tensor_copy(nb[:], nbi[:]), a)
    a = dv(lambda e: e.tensor_copy(bend[:, 0:1], nb[:, 0:1]), a)
    for x in range(1, NR_):
        a = dv(lambda e, x=x: e.tensor_tensor(bend[:, x:x + 1], bend[:, x - 1:x], nb[:, x:x + 1], ALU.add), a)
    dv(lambda e: e.tensor_scalar_add(tot[:], bend[:, NR_ - 1:NR_], -1.0), a)
    a = dv(lambda e: e.tensor_tensor(ysh[:], bend[:], nb[:], ALU.subtract), a)
    a = dv(lambda e: e.tensor_scalar_mul(ysh[:], ysh[:], 128.0), a)
    a = dv(lambda e: e.tensor_tensor(ysh[:], ysh[:], first[:], ALU.subtract), a)
    a = dv(lambda e: e.tensor_scalar(dl[:], nb[:], -1.0, float(CB + 4096), ALU.mult, ALU.add), a)
    a = dv(lambda e: e.tensor_scalar(jt[:, 0], jf[:], tot[0:1, :], None, ALU.min), a)
    sums = [dv(lambda e: e.tensor_copy(jt[:, 1], jt[:, 0]), a)] * 2
    mask = None
    for x in range(NR_):
        prev = mask
        if x < NR_ - 1:
            mask = dv(lambda e, x=x: e.tensor_scalar(jt[:, 2 + x % 2], jt[:, 0], bend[0:1, x:x + 1], dl[0:1, x:x + 1],
                                                     ALU.is_ge, ALU.mult), a, sums[-1])
        if x:
            sums.append(dv(lambda e, x=x: e.tensor_tensor(jt[:, 1], jt[:, 1], jt[:, 2 + (x - 1) % 2], ALU.add),
                           prev, sums[-1]))
    a = dv(lambda e: e.tensor_copy(tabI[:], jt[:, 1]), sums[-1])
    b = dv(lambda e: e.tensor_single_scalar(tabE[:], tabI[:], 12, ALU.arith_shift_right), a)
    dv(lambda e: e.tensor_single_scalar(tabE[:], tabE[:], E - 1, ALU.bitwise_and), b)
    tabs = dv(lambda e: e.tensor_single_scalar(tabR[:], tabI[:], 4095, ALU.bitwise_and), a)
    after = {}

    def results():
        a = tabs
        for x in range(E):
            for p in range(H):
                tt = slice(4 * cuts[p], 4 * cuts[p + 1])
                last_ = dv(lambda e, x=x, tt=tt, r=E * p + x: e.tensor_scalar(
                    T1[:, tt], EX[:, tt], float(x), ysh[:, r:r + 1], ALU.is_equal, ALU.mult), a, dve.last())
            a = last_
            a = dv(lambda e: e.tensor_tensor(P[:], P[:], T1[:], ALU.add), a)
        rows = dv(lambda e: e.tensor_copy(yi[:], P[:]), a)
        a = dv(lambda e: e.tensor_tensor(G[:, :, 1], M[:, :, 1], M[:, :, 0], ALU.subtract), a)
        a = act.do(lambda e: e.activation(G[:, :, 1], G[:, :, 1], ACT.Exp), a)
        a = dv(lambda e: e.tensor_scalar(T1[:, :, 0], G[:, :, 1], 2.0, 2.0, ALU.mult, ALU.add), a, rows)
        a = dv(lambda e: e.reciprocal(G[:, :, 0], T1[:, :, 0]), a)
        gates = dv(lambda e: e.tensor_tensor(G[:, :, 1], G[:, :, 1], G[:, :, 0], ALU.mult), a)
        after["rows"], after["gates"] = rows, gates
        if tables:
            sp.dma(s_w, tables[0], yi[:], rows)
            sp.dma(s_w, tables[1], G[:], gates)

    NX, NYB = 8, 6
    xb_ = X[:].rearrange("p a b d -> p (a b) d")
    xg, yb, sg, hb = xb_[:, 0:NX], xb_[:, NX:NX + NYB], xb_[:, 14:16], xb_[:, 16:18]
    xgT = sb("xgT", [128, 3, 2, 256], F32R)
    hT = sb("hT", [128, 2, 2, 256], F32R)
    s_xg = [c.stream(f"{tag}xg{i}") for i in range(NX)]
    s_yo = [c.stream(f"{tag}yo{i}") for i in range(NYB)]
    bk = c.bank
    tx = Ring([bk[0], bk[1]])
    gu = Ring([bk[2], bk[3]])
    th = Ring([bk[4], bk[5]])
    yk = Ring([bk[6], bk[7]])
    rE, rR = {}, {}
    n_tr = {}
    xl, xtd, gud, htd, hd, trh = {}, {}, {}, {}, {}, {}
    dwn = {}
    ydone = {}
    pe_regs = {}
    quiet = [tabs, act.last(), pe.last(), *scattered]

    def xload(j):
        def f(e):
            r = e.value_load(tabR[0:1, j:j + 1], min_val=0, max_val=NR_ * CB - 1)
            return e.dma_start(xg[:, j % NX], xs[bass.ds(r * 128, 128), :])
        sp.do(f, tabs, *quiet, n_tr.get(j - NX), mark=False)
        wts, f, _ = sp.items[-1]
        sp.items[-1] = (wts, f, (s_xg[j % NX].sem, 16))
        xl[j] = s_xg[j % NX].count()

    def trx(j):
        i, bank, free = tx.take()
        for k in range(2):
            tok = c.tr(bank[:, 128 * k:128 * k + 128], xg[:, j % NX, 128 * k:128 * k + 128], ident[:], xl[j], free, *quiet)
        n_tr[j] = tok
        hi = act.do(lambda e: e.activation(xgT[:, j % 3, 0], bank[:, 0:256], ACT.Copy), tok, gud.get(j - 3))
        tx.free[i] = xtd[j] = dv(lambda e: e.tensor_tensor(
            xgT[:, j % 3, 1], bank[:, 0:256], xgT[:, j % 3, 0].bitcast(F32), ALU.subtract), hi, gud.get(j - 3))

    def gate_up(j):
        def f(e):
            r = e.value_load(tabE[0:1, j:j + 1], min_val=0, max_val=E - 1)
            rE[j] = r
            return None
        pe.do(f, tabs, mark=False)
        i, bank, free = gu.take()
        for k, (p, q) in enumerate(HALVES):
            tok = pe.do(lambda e, k=k, p=p, q=q, bank=bank: e.matmul(
                bank, xgT[:, j % 3, p, 128 * (k // 3):128 * (k // 3) + 128], wgu[q][:, k // 3, bass.ds(rE[j] * 512, 512)],
                start=(k == 0), stop=(k == 5)), xtd[j], free, wl)
        gud[j] = tok
        a = act.do(lambda e: e.activation(sg[:, j % 2], bank[:, 0:256], ACT.Silu), tok, hd.get(j - 2), quiet[2])
        hd[j] = gu.free[i] = dv(lambda e: e.tensor_tensor(hb[:, j % 2], sg[:, j % 2], bank[:, 256:512], ALU.mult), a,
                                trh.get(j - 2))

    def trh_(j):
        i, bank, free = th.take()
        for k in range(2):
            tok = c.tr(bank[:, 128 * k:128 * k + 128], hb[:, j % 2, 128 * k:128 * k + 128], ident[:], hd[j], free)
        trh[j] = tok
        hi = dv(lambda e: e.tensor_copy(hT[:, j % 2, 0], bank[:, 0:256]), tok, dwn.get(j - 2))
        th.free[i] = htd[j] = dv(lambda e: e.tensor_tensor(
            hT[:, j % 2, 1], bank[:, 0:256], hT[:, j % 2, 0].bitcast(F32), ALU.subtract), hi)

    def down(j):
        i, bank, free = yk.take()
        for k, (p, q) in enumerate(HALVES):
            tok = pe.do(lambda e, k=k, p=p, q=q, bank=bank: e.matmul(
                bank[:, 0:D], hT[:, j % 2, p, 128 * (k // 3):128 * (k // 3) + 128], wdn[q][:, k // 3, bass.ds(rE[j] * D, D)],
                start=(k == 0), stop=(k == 5)), htd[j], free)
        dwn[j] = tok
        eng = act
        cp = lambda e: e.activation(yb[:, j % NYB], bank[:, 0:D], ACT.Copy)
        a = yk.free[i] = eng.do(cp, tok, s_yo[j % NYB].last())
        ydone[j] = sp.dma(s_yo[j % NYB], ys[128 * j:128 * j + 128, :], yb[:, j % NYB], a)

    NB = 2 * NT + NR_
    NB0 = 8 * cuts[1] + E
    CBF = 3
    if not tables:
        Xc = xb_[:, 20:32].rearrange("p (a b) d -> p a b d", b=4)
        Y = sb("Y", [128, CBF, 8, D])
        s_cl = [c.stream(f"{tag}cl{i}") for i in range(CBF)]
        s_cg = [c.stream(f"{tag}cg{i}") for i in range(CBF)]
        s_co = [c.stream(f"{tag}co{i}") for i in range(CBF)]
    added = {}

    def fetch(g, *after_):
        z = g % CBF
        ld = sp.dma(s_cl[z], Xc[:, z], xv[g], *quiet, s_co[z].last())
        for t in range(4):
            for k in range(2):
                pool.do(lambda e, t=t, k=k, g=g, z=z: e.indirect_dma_start(
                    Y[:, z, 2 * t + k, :], None, ys[0:128 * (NB if g >= cuts[-2] else NB0), :],
                    bass.IndirectOffsetOnAxis(ap=yi[:, 4 * g + t, k:k + 1], axis=0)), *after_, after["rows"],
                    added.get(g - CBF), mark=False)
                wts, f, _ = pool.items[-1]
                pool.items[-1] = (wts, f, (s_cg[z].sem, 16))
                got = s_cg[z].count()
        return ld, got

    def add(g, ld, got):
        z = g % CBF
        for t in range(4):
            a = dv(lambda e, t=t, z=z, g=g: e.scalar_tensor_tensor(
                Xc[:, z, t], Y[:, z, 2 * t], G[:, 4 * g + t, 0:1], Xc[:, z, t], ALU.mult, ALU.add), ld, got, after["gates"])
        for t in range(4):
            a2 = dv(lambda e, t=t, z=z, g=g: e.scalar_tensor_tensor(
                Xc[:, z, t], Y[:, z, 2 * t + 1], G[:, 4 * g + t, 1:2], Xc[:, z, t], ALU.mult, ALU.add), a)
        added[g] = a2

    def combine(groups, *after_):
        got = {}
        for g in [*groups, None, None]:
            if g is not None:
                got[g] = fetch(g, *after_)
            yield
            n = len(got)
            if g is not None and g - 1 in got:
                add(g - 1, *got[g - 1])
            if g is None and groups[-1] not in added:
                add(groups[-1], *got[groups[-1]])
            for q in groups:
                if q in added and q not in stored and (q + 1 in added or g is None):
                    stored.add(q)
                    sp.dma(s_co[q % CBF], ov[q], Xc[:, q % CBF], added[q])

    stored = set()
    early = iter(())
    for j in range(min(NX, NB)):
        xload(j)
    trx(0)
    trx(1)
    for j in range(NB + 2):
        if j < NB:
            gate_up(j)
        if j == 4:
            results()
        if 1 <= j < NB + 1:
            trh_(j - 1)
        if j + 2 < NB:
            trx(j + 2)
        if j >= 2:
            down(j - 2)
        if j + NX < NB:
            xload(j + NX)
        if H > 1 and j == NB0 + 3:
            early = combine(range(cuts[1]), *[s.last() for s in s_yo])
        if j % 4 == 0:
            next(early, None)

    if tables:
        ctx.close()
        return [s.last() for s in (s_w, *s_yo)]
    for _s in early:
        pass
    yall = [s.last() for s in s_yo]
    for _s in combine(range(cuts[-2], NG), *yall):
        pass
    ctx.close()
    return [s.last() for s in s_co]


def attention(c, B, x0, ys, tables, x1, x2, parts, mdram, cst, w):
    nc, pe, dve, act, pool, sp = c.nc, c.pe, c.dve, c.act, c.pool, c.sp
    ctx = ExitStack()

    def sb(name, shape, dt=F32):
        return ctx.enter_context(nc.sbuf_tensor("at_" + name, shape, dt))

    qst = sb("qst", [99, NS, 2, S], BF16)
    kst = sb("kst", [99, NS, 2, S], BF16)
    P = sb("P", [128, NP, 512])
    NSD = 40
    Sd = sb("Sd", [128, NSD, 128])
    V = sb("V", [128, 2, 8, H, 17])
    XR = sb("XR", [128, 8, D])
    xT = sb("xT", [128, 2, S])
    lat = sb("lat", [DL, S])
    pt = sb("pt", [128, 2, 3, 512], BF16)
    qf = sb("qf", [128, 2, 512])
    OT = sb("OT", [128, 8, D])
    OF = sb("OF", [128, 2, 512])
    Ou = sb("Ou", [128, 2, 512])
    res = sb("res", [128, NR, D])
    ident = sb("ident", [128, 128])
    decn = sb("decn", [128, 512])
    decp = sb("decp", [128, 512])
    Dm = sb("Dm", [128, 128])
    wq = sb("wq", [128, 2, D])
    wk = sb("wk", [128, 2, D])
    wo = sb("wo", [128, 2, D])
    wd = sb("wd", [128, 2, DL])
    wuk = sb("wuk", [DL, D])
    wuv = sb("wuv", [DL, D])
    wkT = Ou[:, 0].rearrange("p (k d) -> p k d", k=2)
    wkv = sb("wkv", [128, 2, DL])
    st = sb("st", [128, 6])
    mv = sb("mv", [128, 8, 2])
    ve = sb("ve", [128, 8])
    sq = sb("sq", [128, 8])
    rs = sb("rs", [128, 8])
    mx = sb("mx", [128, 4, 8, 3])
    m = sb("m", [128, 4, 8])
    mT = sb("mT", [8, 2, 128])
    mp = sb("mp", [8, 2, 3, 128], BF16)
    rc = sb("rc", [128, 4, 4])

    yib = sb("yib", [128, 8, 2], U32)
    gab = sb("gab", [128, 8, 2])
    s_w, s_x, s_y, s_x1 = (c.stream("at_" + n) for n in ("w", "x", "y", "x1"))
    s_m = [c.stream(f"at_m{i}") for i in range(2)]
    s_pt = [c.stream(f"at_pt{i}") for i in range(2)]
    s_st = [c.stream(f"at_st{i}") for i in range(NS)]
    s_mr = [c.stream(f"at_mr{i}") for i in range(NS)]
    s_res = [c.stream(f"at_res{i}") for i in range(NR)]
    s_yr = [c.stream(f"at_yr{i}") for i in range(NR)]

    def fold(a):
        return a.rearrange("(k p) n -> p k n", p=128)

    for dst, src in ((ident[:], cst["ident"]), (decn[:], cst["decn"]), (decp[:], cst["decp"]),
                     (Dm[:], cst["dm"]), (wq[:], fold(w["q"])), (wk[:], fold(w["k"])),
                     (wkT, fold(w["v"])), (wd[:], fold(w["down"])), (wuk[:], w["upk"]),
                     (wuv[:], w["upv"]), (wo[:], fold(w["o"]))):
        loaded = sp.dma(s_w, dst, src)
    ones_k = dve.do(lambda e: e.memset(kst[96:99, :, :, :], 1.0))
    ones_v = dve.do(lambda e: e.memset(V[:, :, :, :, 16:17], 1.0))
    v0 = dve.do(lambda e: e.memset(c.V, 0.0))
    wsum = dve.do(lambda e: e.tensor_tensor(wk[:], wk[:], wkT, ALU.add), loaded)
    wqs = dve.do(lambda e: e.tensor_scalar_mul(wq[:], wq[:], 1.0 / 16.0), loaded)
    fT = {}
    for i in range(2):
        def fill(bank, free, i=i):
            for j in range(2):
                t = c.tr(bank[:, 128 * j:128 * j + 128], wk[:, i, 128 * j:128 * j + 128], ident[:],
                         wsum, loaded, free)
            return t

        def use(bank, tok, i=i):
            fT[i] = dve.do(lambda e: e.tensor_copy(
                Ou[:, 0].rearrange("p (j i q) -> p j i q", j=2, i=2)[:, :, i, :],
                bank[:, 0:256].rearrange("p (j q) -> p j q", j=2)), tok, wsum)
            return fT[i]
        c.unit(fill, use)

    def fill_wkv(bank, free):
        for i in range(2):
            for j in range(2):
                t = c.mm(bank[:, i * DL:(i + 1) * DL], Ou[:, 0, 256 * j + 128 * i:256 * j + 128 * i + 128],
                         wd[:, j, :], fT[0], fT[1], free, start=(j == 0), stop=(j == 1))
        return t

    def use_wkv(bank, tok):
        return dve.do(lambda e: e.tensor_copy(wkv[:], bank[:, 0:128].rearrange("p (k n) -> p k n", k=2)), tok)
    c.unit(fill_wkv, use_wkv)
    setup = dve.last()

    xdone = {}
    vdone = {}
    pdone = {}
    vread = {}

    xl = {}

    def xload(b, *after):
        sp.dma(s_x, XR[:], x0[b].rearrange("(t p) d -> p t d", p=128), *after)
        sp.dma(s_x, yib[:], tables[0][:, 8 * b:8 * b + 8, :], added.get(b - 1))
        xl[b] = sp.dma(s_x, gab[:], tables[1][:, 8 * b:8 * b + 8, :], added.get(b - 1))
        return xl[b]

    added, x1s = {}, {}
    rows = xT[:].rearrange("p k (t d) -> p (k t) d", d=D)

    def combine(b):
        ld = xload(b) if b == 0 else xl[b]
        for half in range(2):
            for t in range(4):
                for k in range(2):
                    pool.do(lambda e, t=t, k=k, half=half: e.indirect_dma_start(
                        rows[:, 2 * t + k, :], None, ys,
                        bass.IndirectOffsetOnAxis(ap=yib[:, 4 * half + t, k:k + 1], axis=0)),
                        ld, prepd.get(b - 1), added.get(b), mark=False)
                    wts, f, _ = pool.items[-1]
                    pool.items[-1] = (wts, f, (s_y.sem, 16))
                    got = s_y.count()
            for _s in range(20):
                yield
            a = None
            for k in range(2):
                for t in range(4):
                    tt = 4 * half + t
                    a = dve.do(lambda e, t=t, tt=tt, k=k: e.scalar_tensor_tensor(
                        XR[:, tt, :], rows[:, 2 * t + k, :], gab[:, tt, k:k + 1], XR[:, tt, :], ALU.mult, ALU.add),
                        got, ld, dve.last() if k and not t else None)
                    if t == 3:
                        yield
            added[b] = a
        x1s[b] = sp.dma(s_x1, x1[b].rearrange("(t p) d -> p t d", p=128), XR[:], added[b])
        for _s in range(3):
            yield

    def prep(b):
        for t in range(8):
            s1 = dve.do(lambda e, t=t: e.bn_stats(st[:], XR[:, t, :]), added[b], dve.last())
            ag = dve.do(lambda e, t=t: e.bn_aggr(mv[:, t, :], st[:]), s1)
            if t % 3 == 2:
                yield
        a = dve.do(lambda e: e.tensor_scalar_add(ve[:], mv[:, :, 1], EPS), ag)
        yield
        yield
        a2 = act.do(lambda e: e.activation(sq[:], ve[:], ACT.Sqrt), a)
        yield
        yield
        a3 = dve.do(lambda e: e.reciprocal(rs[:], sq[:]), a2)
        n1 = dve.do(lambda e: e.tensor_tensor(sq[:], rs[:], rs[:], ALU.mult), a3)
        n2 = dve.do(lambda e: e.tensor_tensor(sq[:], sq[:], ve[:], ALU.mult), n1)
        n3 = dve.do(lambda e: e.tensor_scalar(sq[:], sq[:], -0.5, 1.5, ALU.mult, ALU.add), n2)
        n4 = dve.do(lambda e: e.tensor_tensor(rs[:], rs[:], sq[:], ALU.mult), n3)
        for t in range(8):
            xn = dve.do(lambda e, t=t: e.tensor_scalar(XR[:, t, :], XR[:, t, :], mv[:, t, 0:1], rs[:, t:t + 1],
                                                       ALU.subtract, ALU.mult), n4, ag, x1s[b])
            if t % 2:
                yield
        yield
        xTd = {}
        for ch in range(2):
            for k in range(2):
                def fill(bank, free, ch=ch, k=k):
                    for t in range(4):
                        tok = c.tr(bank[:, 128 * t:128 * t + 128], XR[:, 4 * ch + t, 128 * k:128 * k + 128],
                                   ident[:], xn, free)
                    return tok

                def use(bank, tok, ch=ch, k=k):
                    xTd[ch] = act.do(lambda e: e.activation(xT[:, k, 512 * ch:512 * ch + 512], bank[:], ACT.Copy),
                                     tok, added[b], prepd.get(b - 1))
                    return xTd[ch]
                c.unit(fill, use)
                yield
        xread = pe.last()
        latd = {}
        for ch in range(2):
            def fill(bank, free, ch=ch):
                for k in range(2):
                    tok = c.mm(bank[0:DL, :], wkv[:, k, :], xT[:, k, 512 * ch:512 * ch + 512], xTd[ch], setup, free,
                               start=(k == 0), stop=(k == 1))
                return tok

            def use(bank, tok, ch=ch):
                latd[ch] = act.do(lambda e: e.activation(lat[:, 512 * ch:512 * ch + 512], bank[0:DL, :], ACT.Copy), tok)
                return latd[ch]
            c.unit(fill, use)
            yield
        for kind in range(2):
            for hf in range(2):
                for ch in range(2):
                    def fill(bank, free):
                        sl = slice(512 * ch, 512 * ch + 512)
                        if kind == 0:
                            for k in range(2):
                                tok = c.mm(bank[:], wq[:, k, 128 * hf:128 * hf + 128], xT[:, k, sl], xTd[ch], wqs, free,
                                           start=(k == 0), stop=(k == 1))
                        else:
                            tok = c.mm(bank[:], wuk[:, 128 * hf:128 * hf + 128], lat[:, sl], latd[ch], free)
                        return tok

                    def use(bank, tok):
                        prev = st_pool.get("q")
                        for v in range(2):
                            st_pool["f"] = act.do(lambda e, v=v, far=far: e.activation(
                                qf[:, v], bank[:], ACT.Copy, scale=far[v]), tok, prev)
                        return st_pool["f"]
                    far = (FAR[ch], FAR[1 - ch])
                    c.unit(fill, use)
                    yield
                    ready = st_pool["f"]
                    a = [pool.do(lambda e, v=v: e.tensor_tensor(qf[:, v], qf[:, v], (decn, decp)[v][:], ALU.mult),
                                 ready, loaded) for v in range(2)]
                    for _s in range(4):
                        yield
                    for p in range(2):
                        for v in range(2):
                            r = act.do(lambda e, v=v, p=p: e.activation(pt[:, v, p, :], qf[:, v], ACT.Copy),
                                       a[v], st_pool.get(("d", v)))
                            a[v] = pool.do(lambda e, v=v, p=p: e.tensor_tensor(
                                qf[:, v] if p == 0 else pt[:, v, 2, :], qf[:, v], pt[:, v, p, :], ALU.subtract), r)
                            yield
                        yield
                    st_pool["q"] = a[1]
                    for v in range(2):
                        for p in range(3):
                            dst = parts[b % 2, kind, 8 * hf:8 * hf + 8, p, :, v, 512 * ch:512 * ch + 512]
                            st_pool[("d", v)] = sp.dma(s_pt[v], dst, pt[:, v, p, :], a[v], stfree.get(b - 2))
        pdone[b] = [s_pt[0].last(), s_pt[1].last()]
        if b + 1 < B:
            xload(b + 1, xread)
        for t2 in range(4):
            def fill(bank, free):
                for j in range(2):
                    t = 2 * t2 + j
                    tok = c.mm(bank[:, 256 * j:256 * j + 256], lat[:, 128 * t:128 * t + 128], wuv[:], latd[t // 4], free)
                return tok

            def use(bank, tok):
                vdone[b] = act.do(lambda e, t2=t2, b=b: e.activation(
                    V[:, b % 2, 2 * t2:2 * t2 + 2, :, 0:16],
                    bank[:].rearrange("p (t h d) -> p t h d", t=2, h=H), ACT.Copy), tok, vread.get(b - 2))
                return vdone[b]
            c.unit(fill, use)
            yield
        prepd[b] = pe.last()

    prepd = {}
    st_pool = {}
    stfree = {}
    filled = {}
    NH = B * H

    def fill_stack(n):
        b, h = divmod(n, H)
        s = n % NS
        free = free_of(n)
        more = [*pdone[b], free]
        src = parts[b % 2]
        qd = qst[:, s, :, :]
        kd = kst[:, s, :, :]
        for p, (r0, r1) in enumerate(((0, 3), (3, 5), (5, 6))):
            for r in range(r0, r1):
                sp.dma(s_st[s], qd[16 * r:16 * r + 16], src[0, h, p], *more)
        sp.dma(s_st[s], kd[0:48], src[1, h].rearrange("p d v t -> (p d) v t"), *more)
        sp.dma(s_st[s], kd[48:80], src[1, h, 0:2].rearrange("p d v t -> (p d) v t"), *more)
        filled[n] = sp.dma(s_st[s], kd[80:96], src[1, h, 0], *more)
        if h == H - 1:
            stfree[b] = filled[n]

    tdone = {}
    sdfree = [None] * NSD
    sdlist = list(range(NSD))
    sdslot = {}
    sdtok = {}
    mrow = {}
    mdone = {}

    def pieces(t, c0, c1, diag_last):
        out = []
        if diag_last:
            left = [(0, 0, 128 * t, 0), (128 * t, 128 * t + 128, 896 - 128 * t, 1), (896, 128 * t, 128, 0)]
        else:
            left = [(0, 0, 128 * t, 0), (128 * t + 128, 128 * t + 128, 896 - 128 * t, 1)]
        for col, key, n, side in left:
            a, z = max(col, c0), min(col + n, c1)
            if z > a:
                out.append((a, key + a - col, z - a, side))
        return out

    def s_stream():
        late = []
        for n in range(NH):
            s, z = n % NS, n % 4
            assert n in filled
            for t in range(8):
                slot = sdlist.pop(0)
                sdslot[(n, t)] = slot
                for u in range(2):
                    def fill(bank, free):
                        for col, key, ln, side in pieces(t, 512 * u, 512 * u + 512, True):
                            tok = c.mm(bank[:, col - 512 * u:col - 512 * u + ln],
                                       qst[0:96, s, side, 128 * t:128 * t + 128],
                                       kst[0:96, s, 1 - side, key:key + ln], filled[n], free)
                        return tok

                    def use(bank, tok, s=s, z=z, t=t, slot=slot):
                        if u == 0:
                            return dve.do(lambda e: e.tensor_reduce(
                                mx[:, z, t, 0:1], bank[:, 0:512], op=ALU.max, axis=AX.X), tok, mdone.get(n - 4))
                        dve.do(lambda e: e.tensor_reduce(
                            mx[:, z, t, 1:2], bank[:, 0:384], op=ALU.max, axis=AX.X), tok)
                        sdtok[(n, t)] = dve.do(lambda e: e.tensor_tensor_reduce(
                            out=Sd[:, slot, :], in0=bank[:, 384:512], in1=Dm[:], scale=1.0, scalar=-3.0e38,
                            op0=ALU.mult, op1=ALU.max, accum_out=mx[:, z, t, 2:3]), tok, sdfree[slot], loaded)
                        return sdtok[(n, t)]
                    c.unit(fill, use)
                    sdone[0] += 1
                    yield
                if late and t in (0, 1, 2):
                    late.pop(0)()
            late = maxima(n)
        for f in late:
            f()

    def maxima(n):
        s, z = n % NS, n % 4
        mdone[n] = dve.do(lambda e: e.tensor_reduce(m[:, z, :], mx[:, z], op=ALU.max, axis=AX.X),
                          sdtok[(n, 7)], mread.get(n - 4))
        for t in range(8):
            slot = sdslot[(n, t)]
            sdtok[(n, t)] = pool.do(lambda e, slot=slot, t=t: e.tensor_tensor(
                Sd[:, slot, :], Sd[:, slot, :], m[:, z, t:t + 1].to_broadcast([128, 128]), ALU.subtract), mdone[n])
        mread[n] = sdtok[(n, 7)]
        y = n % 2
        t0 = {}

        def turn():
            def fill(bank, free):
                mt = c.tr(bank[0:8, 0:128], m[:, z, :], ident[:], mdone[n], free)
                mreadpe[n] = mt
                return mt

            def use(bank, tok):
                t0[0] = dve.do(lambda e: e.tensor_scalar_mul(mT[:, y], bank[0:8, 0:128], -1.0), tok)
                return t0[0]
            c.unit(fill, use)

        def split():
            t1 = dve.do(lambda e: e.tensor_copy(mp[:, y, 0, :], mT[:, y]), t0[0], wrote.get(n - 2))
            t2 = dve.do(lambda e: e.tensor_tensor(mT[:, y], mT[:, y], mp[:, y, 0, :], ALU.subtract), t1)
            t3 = dve.do(lambda e: e.tensor_copy(mp[:, y, 1, :], mT[:, y]), t2)
            t0[1] = dve.do(lambda e: e.tensor_tensor(mp[:, y, 2, :], mT[:, y], mp[:, y, 1, :], ALU.subtract), t3)

        def send():
            wrote[n] = sp.dma(s_m[y], mdram[z], mp[:, y], t0[1], mrow.get(n - 4))
            for v in range(2):
                mrow[n] = sp.dma(s_mr[s], qst[96:99, s, v, :].rearrange("c (t q) -> c t q", q=128),
                                 mdram[z].rearrange("t c q -> c t q"), wrote[n], free_of(n))
        return [turn, split, send]

    def free_of(n):
        return tdone[(n - NS) // 4] if n >= NS else None

    mread, mreadpe, wrote = {}, {}, {}
    sdone = [0]
    pfree = [None] * NP
    pvfree = [v0]
    late_work = []

    def t_stream():
        pn = tn = 0
        nt = len(c.T)
        ready, bufs = [], []
        tfree = [None] * nt
        for g in range(NH // 4):
            for qh in range(2):
                for kk in range(8):
                    kb = (kk + 4 * qh) % 8
                    for hh in range(4):
                        n = 4 * g + hh
                        s = n % NS
                        i = tn % nt
                        tn += 1
                        bank = c.T[i]
                        tok = None
                        for col, q0, ln, side in pieces(kb, 512 * qh, 512 * qh + 512, False):
                            col -= 512 * qh
                            tok = c.mm(bank[:, col:col + ln], kst[0:99, s, side, 128 * kb:128 * kb + 128],
                                       qst[0:99, s, 1 - side, q0:q0 + ln], filled[n], mrow[n], ones_k, tfree[i])
                        if kb // 4 == qh:
                            slot = sdslot[(n, kb)]
                            col = 128 * (kb % 4)
                            tok = c.tr(bank[:, col:col + 128], Sd[:, slot, :], ident[:], sdtok[(n, kb)], tfree[i])
                            sdfree[slot] = tok
                            sdlist.append(slot)
                        pi = pn % NP
                        pn += 1
                        ex = act.do(lambda e, pi=pi, bank=bank: e.activation(P[:, pi, :], bank, ACT.Exp), tok, pfree[pi])
                        tfree[i] = ex
                        bufs.append((pi, ex))
                        if kk == 7 and hh == 3 and qh == 1:
                            tdone[g] = tok
                        yield g
                        if ready and hh == 1:
                            weigh(*ready)
                            ready = []
                    ready, bufs = [g, qh, kk, kb, bufs], []
        weigh(*ready)

    def weigh(g, qh, kk, kb, pv):
        b = g // 4
        for hh in range(4):
            pi, ex = pv[hh]
            h = (4 * g + hh) % H
            tok = pfree[pi] = c.mm(c.V[32 * hh:32 * hh + 17, :], V[:, b % 2, kb, h, :], P[:, pi, :],
                                   ex, vdone[b], ones_v, pvfree[0], start=(kk == 0), stop=(kk == 7))
        if kk == 7:
            vread[b] = tok
            assert (g, qh) in oread or not g
            pvfree[0] = act.do(lambda e: e.activation(Ou[:, qh], c.V, ACT.Copy), tok, wfold[("o", qh)])
            late_work.append(normed(g, qh, pvfree[0]))

    def normed(g, qh, ev):
        b = g // 4

        def fill(bank, free):
            for t in range(4):
                tok = c.tr(bank[:, 128 * t:128 * t + 128], Ou[:, qh, 128 * t:128 * t + 128], ident[:], ev, free)
            wfold[("o", qh)] = tok
            oread.add((g + 1, qh))
            return tok

        def use(bank, tok):
            v4 = bank.rearrange("p (t h x) -> p t h x", t=4, h=4)
            r1 = dve.do(lambda e: e.reciprocal(rc[:], v4[:, :, :, 16]), tok, wfold.get("rc"))
            g4 = 64 * (g % 4)
            wfold["rc"] = dve.do(lambda e: e.tensor_tensor(
                OT[:, 4 * qh:4 * qh + 4, g4:g4 + 64].rearrange("p t (h x) -> p t h x", h=4),
                v4[:, :, :, 0:16], rc[:].rearrange("p t (h o) -> p t h o", o=1).to_broadcast([128, 4, 4, 16]),
                ALU.mult), r1, wfold.get("otr"))
            return wfold["rc"]
        c.unit(fill, use)
        yield
        if g % 4 < 3 or qh == 0:
            return
        otd = wfold["rc"]
        resl = {}

        def resload(tt):
            r = tt % NR
            resl[tt] = sp.dma(s_res[r], res[:, r, :], x1[b, 128 * tt:128 * tt + 128, :], x1s[b], s_yr[r].last())
        for tt in range(NR):
            resload(tt)
        for ch in range(2):
            for k in range(2):
                def fill(bank, free):
                    for t in range(4):
                        tok = c.tr(bank[:, 128 * t:128 * t + 128], OT[:, 4 * ch + t, 128 * k:128 * k + 128],
                                   ident[:], otd, free)
                    wfold["otr"] = tok
                    return tok

                def use(bank, tok):
                    wfold["of"] = act.do(lambda e, k=k: e.activation(OF[:, k, :], bank[:], ACT.Copy), tok, wfold.get("pj"))
                    return wfold["of"]
                c.unit(fill, use)
                yield
            for t in range(4):
                tt = 4 * ch + t
                r = tt % NR
                ld = resl.pop(tt)

                def fill(bank, free):
                    for k in range(2):
                        tok = c.mm(bank[:, 0:D], OF[:, k, 128 * t:128 * t + 128], wo[:, k, :], wfold["of"], free,
                                   start=(k == 0), stop=(k == 1))
                    wfold["pj"] = tok
                    return tok

                def use(bank, tok):
                    rr = dve.do(lambda e, r=r: e.tensor_tensor(res[:, r, :], bank[:, 0:D], res[:, r, :], ALU.add), tok, ld)
                    sp.dma(s_yr[r], x2[b, 128 * tt:128 * tt + 128, :], res[:, r, :], rr)
                    return rr
                c.unit(fill, use)
                yield
                if 0 < tt and tt - 1 + NR < 8:
                    resload(tt - 1 + NR)

    wfold = {("o", 0): setup, ("o", 1): setup}
    oread = set()

    for work in (combine(0), prep(0)):
        for _ in work:
            pass
    nf = 0
    while nf < min(NS, NH):
        if nf // H not in pdone:
            break
        fill_stack(nf)
        nf += 1
    ss = s_stream()
    LEAD = 8
    ahead = [(f(b), 64 * (4 * b - back) + at) for b in range(1, B) for f, back, at in ((combine, 6, 0), (prep, 5, -8))]

    def advance():
        if next(ahead[0][0], 1) == 1:
            ahead.pop(0)

    while sdone[0] < min(2 * (32 + LEAD), 16 * NH):
        next(ss)
        if ahead:
            advance()
    step = 0
    for g in t_stream():
        if step % 64 in (4, 16, 28, 44) and g and nf < NH:
            while nf // H not in pdone:
                advance()
            fill_stack(nf)
            nf += 1
        due = len(ahead) and step >= ahead[0][1]
        next(ss, None)
        if due and step % 8 not in (1, 3, 5):
            advance()
        elif late_work and (step % 4 == 1 or not due) and next(late_work[0], 1) == 1:
            late_work.pop(0)
        step += 1
    for _ in ss:
        pass
    for w_ in late_work:
        for _ in w_:
            pass
    ctx.close()
    return [s.last() for s in s_yr]


def consts():
    t = np.arange(S, dtype=np.float64) - (S / 4 - 0.5)
    i = np.arange(128, dtype=np.float64)
    return {
        "tri": (i[:, None] < i[None, :]).astype(np.float32),
        "misc": np.concatenate([np.tile(np.arange(16), (128, 1)), i[:, None]], 1).astype(np.float32),
        "jf": np.arange(NBLK, dtype=np.float32)[None, :],
        "ident": np.eye(128, dtype=np.float32),
        "decn": np.tile(np.exp(-LAM * t[:512]).astype(np.float32), (128, 1)),
        "decp": np.tile(np.exp(LAM * t[:512]).astype(np.float32), (128, 1)),
        "dm": np.exp(np.minimum(0.0, 2 * LAM * (i[:, None] - i[None, :]))).astype(np.float32),
    }


_INS = ['L0_attn_x', 'L0_attn_W_q', 'L0_attn_W_k', 'L0_attn_W_v', 'L0_attn_W_o', 'L0_attn_W_down_kv', 'L0_attn_W_up_k',
        'L0_attn_W_up_v', 'L0_ffn_router_w', 'L0_ffn_router_b', 'L0_ffn_we_gate', 'L0_ffn_we_up', 'L0_ffn_we_down']
_ROUTE = ("ident", "tri", "misc", "jf")


def program(nc, a, cst, out):
    B = 16
    x, wq, wk, wv, wo, wdn, wuk, wuv, rw, rb, eg, eu, ed = a
    with ExitStack() as ctx:
        c = Core(nc, ctx)
        x1 = nc.dram_tensor("x1", [B, S, D], F32).ap()
        x2 = nc.dram_tensor("x2", [B, S, D], F32).ap()
        xs = nc.dram_tensor("xs", [XROWS, D], F32).ap()
        ys = nc.dram_tensor("ys", [NBLK * 128, D], F32).ap()
        parts = nc.dram_tensor("parts", [2, 2, H, 3, HD, 2, S], BF16).ap()
        mdram = nc.dram_tensor("mdram", [4, 8, 3, 128], BF16).ap()
        tables = [nc.dram_tensor(f"table{i}", [128, B * S // 128, 2], dt).ap() for i, dt in enumerate((U32, F32))]
        we = {"rw": rw, "rb": rb, "g": eg, "u": eu, "d": ed}
        wa = {"q": wq, "k": wk, "v": wv, "o": wo, "down": wdn, "upk": wuk, "upv": wuv}

        def flat(t):
            return t.rearrange("b s d -> (b s) d")
        moe(c, B * S // 128, flat(x), None, xs, ys, cst, we, [], "m1", tables)
        c.meet()
        attention(c, B, x, ys[0:128 * 264, :], tables, x1, x2, parts, mdram, cst, wa)
        c.meet()
        moe(c, B * S // 128, flat(x2), flat(out), xs, ys, cst, we, [], "m2", cuts=(22,))
        ends = [s.last() for s in c.streams if s.n]
        block = ctx.enter_context(nc.Block())

        @block.sync
        def _(e):
            c.sp.run(e)
            for sem, n, _k in ends:
                e.wait_ge(sem, n)

        @block.scalar
        def _(e):
            c.act.run(e)

        @block.vector
        def _(e):
            c.dve.run(e)

        @block.tensor
        def _(e):
            c.pe.run(e)

        @block.gpsimd
        def _(e):
            c.pool.run(e)


def kernel(**inputs):
    import concourse.bacc as _bacc
    from concourse.bass_utils import run_bass_kernel_spmd as _run

    nc = _bacc.Bacc("TRN2", target_bir_lowering=False, num_devices=1)
    arrays, args = {}, []
    for name in _INS:
        v = np.ascontiguousarray(inputs[name])
        arrays[f"in_{name}"] = v
        args.append(nc.dram_tensor(f"in_{name}", v.shape, mybir.dt.from_np(v.dtype), kind="ExternalInput").ap())
    cst = {}
    for name, v in consts().items():
        arrays[f"const_{name}"] = v
        cst[name] = nc.dram_tensor(f"const_{name}", v.shape, F32, kind="ExternalInput").ap()
    out = nc.dram_tensor("out", (16, S, D), F32, kind="ExternalOutput").ap()
    program(nc, args, cst, out.rearrange("b s d -> b s d"))
    r = _run(nc, [arrays], core_ids=[0])
    return r.results[0]["out"]
```
